# Optimizing a Trainium2 kernel written in Bass

```python
import numpy as np
import jax
import jax.numpy as jnp

def _softmax(x, axis=-1):
    return jax.nn.softmax(x, axis=axis)

def _gelu(x):
    return jax.nn.gelu(x, approximate=True)

def _silu(x):
    return jax.nn.silu(x)

def _sigmoid(x):
    return jax.nn.sigmoid(x)

def _layernorm(x, axis=-1, eps=1e-05):
    m = jnp.mean(x, axis=axis, keepdims=True)
    v = jnp.var(x, axis=axis, keepdims=True)
    return (x - m) / jnp.sqrt(v + eps)

def _scatter_add(tgt, idx, src, axis=0):
    return tgt.at[idx].add(src)

def _segment_sum(src, seg, n):
    return jax.ops.segment_sum(src, seg, n)
kernel_name = 'mk_seq_preln_d1_jaxref_r4_5b5533'

def setup_inputs(seed: int=0):
    np.random.seed(seed)
    _w = jnp.asarray

    def _L0_attn_setup():
        import jax, jax.numpy as jnp
        import numpy as np
        H = 16

        def _pairwise_l2(pos):
            sq = jnp.sum((pos[:, :, None, :] - pos[:, None, :, :]) ** 2, axis=-1)
            safe = jnp.where(sq > 0, sq, 1.0)
            return jnp.where(sq > 0, jnp.sqrt(safe), 0.0)
        key = jax.random.key(seed)
        ks = jax.random.split(key, 12)
        B, S, D = (2, 512, 256)
        init = lambda k, shape: jax.random.normal(k, shape, dtype=jnp.float32) * 0.02
        return {'x': jax.random.normal(ks[0], (B, S, D), dtype=jnp.float32), 'wq': init(ks[1], (D, D)), 'bq': init(ks[2], (D,)), 'wk': init(ks[3], (D, D)), 'bk': init(ks[4], (D,)), 'wv': init(ks[5], (D, D)), 'bv': init(ks[6], (D,)), 'wo': init(ks[7], (D, D)), 'bo': init(ks[8], (D,)), 'w3d': init(ks[9], (3, D)), 'b3d': init(ks[10], (3,))}
    _L0_attn_in = _L0_attn_setup()

    def _L0_ffn_setup():
        import jax, jax.numpy as jnp
        import numpy as np
        import math
        D_IN = 256
        FEATURES = (1024, 1024, 256)
        BATCH, SEQ = (8, 512)

        def _conn_dense(kernel_bool, x):
            w = jnp.where(kernel_bool, jnp.float32(1.0), jnp.float32(-1.0))
            return x @ w
        key = jax.random.key(seed)
        kx, kk0, kk1, kk2 = jax.random.split(key, 4)
        x = jax.random.normal(kx, (BATCH, SEQ, D_IN), dtype=jnp.float32)
        k0 = jax.random.randint(kk0, (2 * D_IN, FEATURES[0]), 0, 2).astype(jnp.bool_)
        k1 = jax.random.randint(kk1, (FEATURES[0], FEATURES[1]), 0, 2).astype(jnp.bool_)
        k2 = jax.random.randint(kk2, (FEATURES[1], FEATURES[2]), 0, 2).astype(jnp.bool_)
        s0 = jnp.asarray(1.0 / math.sqrt(2 * D_IN), dtype=jnp.float32)
        s1 = jnp.asarray(1.0 / math.sqrt(FEATURES[0]), dtype=jnp.float32)
        s2 = jnp.asarray(1.0 / math.sqrt(FEATURES[1]), dtype=jnp.float32)
        return {'x': x, 'k0': k0, 'k1': k1, 'k2': k2, 's0': s0, 's1': s1, 's2': s2}
    _L0_ffn_in = _L0_ffn_setup()
    _d = {'L0_attn_x': _L0_attn_in['x'], 'L0_attn_wq': _L0_attn_in['wq'], 'L0_attn_bq': _L0_attn_in['bq'], 'L0_attn_wk': _L0_attn_in['wk'], 'L0_attn_bk': _L0_attn_in['bk'], 'L0_attn_wv': _L0_attn_in['wv'], 'L0_attn_bv': _L0_attn_in['bv'], 'L0_attn_wo': _L0_attn_in['wo'], 'L0_attn_bo': _L0_attn_in['bo'], 'L0_attn_w3d': _L0_attn_in['w3d'], 'L0_attn_b3d': _L0_attn_in['b3d'], 'L0_ffn_k0': _L0_ffn_in['k0'], 'L0_ffn_k1': _L0_ffn_in['k1'], 'L0_ffn_k2': _L0_ffn_in['k2'], 'L0_ffn_s0': _L0_ffn_in['s0'], 'L0_ffn_s1': _L0_ffn_in['s1'], 'L0_ffn_s2': _L0_ffn_in['s2']}
    _x0 = _d['L0_attn_x']
    _d['L0_attn_x'] = jax.random.normal(jax.random.fold_in(jax.random.key(seed), 1), (8, 512, 256), dtype=_x0.dtype)
    del _x0
    return _d

def reference(L0_attn_x, L0_attn_wq, L0_attn_bq, L0_attn_wk, L0_attn_bk, L0_attn_wv, L0_attn_bv, L0_attn_wo, L0_attn_bo, L0_attn_w3d, L0_attn_b3d, L0_ffn_k0, L0_ffn_k1, L0_ffn_k2, L0_ffn_s0, L0_ffn_s1, L0_ffn_s2):

    def _L0_attn_ref(x, wq, bq, wk, bk, wv, bv, wo, bo, w3d, b3d):
        import jax, jax.numpy as jnp
        import numpy as np
        H = 16

        def _pairwise_l2(pos):
            sq = jnp.sum((pos[:, :, None, :] - pos[:, None, :, :]) ** 2, axis=-1)
            safe = jnp.where(sq > 0, sq, 1.0)
            return jnp.where(sq > 0, jnp.sqrt(safe), 0.0)
        B, S, D = x.shape
        hd = D // H
        scale = 1.0 / hd ** 0.5
        V = (x @ wv.T + bv).reshape(B, S, H, hd).transpose(0, 2, 1, 3)
        pos = x @ w3d.T + b3d
        dist = _pairwise_l2(pos)
        scores = -dist[:, None, :, :] * scale
        causal = jnp.triu(jnp.ones((S, S), dtype=bool), k=1)
        scores = jnp.where(causal[None, None], -jnp.inf, scores)
        attn = jax.nn.softmax(scores, axis=-1)
        attn = jnp.nan_to_num(attn, nan=0.0)
        out = jnp.einsum('bhqk,bhkd->bhqd', attn, V)
        out = out.transpose(0, 2, 1, 3).reshape(B, S, D)
        return out @ wo.T + bo

    def _L0_ffn_ref(x, k0, k1, k2, s0, s1, s2):
        import jax, jax.numpy as jnp
        import numpy as np
        import math
        D_IN = 256
        FEATURES = (1024, 1024, 256)
        BATCH, SEQ = (8, 512)

        def _conn_dense(kernel_bool, x):
            w = jnp.where(kernel_bool, jnp.float32(1.0), jnp.float32(-1.0))
            return x @ w
        h = jnp.concatenate([x, -x], axis=-1)
        h = s0 * _conn_dense(k0, h)
        h = jax.nn.relu(h) * 2
        h = s1 * _conn_dense(k1, h)
        h = jax.nn.relu(h) * 2
        h = s2 * _conn_dense(k2, h)
        return h
    x = L0_attn_x
    x = x + _L0_attn_ref(_layernorm(x, axis=-1), L0_attn_wq, L0_attn_bq, L0_attn_wk, L0_attn_bk, L0_attn_wv, L0_attn_bv, L0_attn_wo, L0_attn_bo, L0_attn_w3d, L0_attn_b3d)
    x = x + _L0_ffn_ref(_layernorm(x, axis=-1), L0_ffn_k0, L0_ffn_k1, L0_ffn_k2, L0_ffn_s0, L0_ffn_s1, L0_ffn_s2)
    return x

_drawn_inputs = setup_inputs


def setup_inputs(seed=0):
    import zlib

    import numpy as np

    out = dict(_drawn_inputs(seed))
    spreads = {}
    factors = {'L0_attn_wv': 4.824,
     'L0_attn_bv': 8.0,
     'L0_attn_wo': 4.188,
     'L0_attn_bo': 3.003,
     'L0_attn_w3d': 8.0,
     'L0_attn_b3d': 8.0}
    for name, (base, spread) in spreads.items():
        noise = np.random.default_rng([zlib.crc32(name.encode()), seed]).standard_normal(out[name].shape)
        drawn = base * np.exp(spread * noise) if base else spread * noise
        out[name] = jnp.asarray(drawn.astype(out[name].dtype))
    for name, factor in factors.items():
        out[name] = (out[name] * factor).astype(out[name].dtype)
    return out
```

```python
from contextlib import ExitStack

import concourse.bass as bass
from concourse import mybir

ALU = mybir.AluOpType
ACT = mybir.ActivationFunctionType
F32 = mybir.dt.float32
F16 = mybir.dt.float16
BF16 = mybir.dt.bfloat16
U8 = mybir.dt.uint8

P = 128
HEADS = 16
EPS = 1e-5
TINY = 2.0 ** -100
XN_SCALE = 2.0 ** 10
W0_SCALE = 2.0 ** -4
W1_SCALE = 2.0 ** -10
OUT_SCALE = 2.0 ** 4 * 4.0
FBANKS = 3


def block_kernel(nc, x, wv, bv, wo, bo, w3d, b3d, k0, k1, k2, s0, s1, s2, out):
    BATCHES, SEQ, D = x.shape
    FF = k1.shape[0]
    NT = SEQ // P
    ND = D // P
    NF = FF // P
    COORDS = w3d.shape[0]
    PARTS = 3
    SCORE_SCALE = 1.0 / (D // HEADS) ** 0.5
    USES = 2 * NF + NT // 2
    VC = D + COORDS
    ROW = [sum(SEQ - j * P for j in range(kt)) for kt in range(NT)]
    NS = ROW[-1] + SEQ - (NT - 1) * P
    CHUNKS = [(0, SEQ), (SEQ, NS)]
    assert USES % FBANKS == 0 and FF == k0.shape[1] and k0.shape[0] == 2 * D

    with ExitStack() as ctx:
        def sb(name, shape, dt):
            return ctx.enter_context(nc.sbuf_tensor(name, shape, dt))

        def psum(name, shape, dt=F32):
            return ctx.enter_context(nc.psum_tensor(name, shape, dt))

        def sem(name):
            return ctx.enter_context(nc.semaphore(name))

        ident = sb("ident", [P, P], F32)
        ident16 = sb("ident16", [P, P], F16)
        identb = sb("identb", [P, P], BF16)
        causal = sb("causal", [P, P], F32)
        pick = sb("pick", [PARTS * COORDS, COORDS, P], BF16)
        neg_half = sb("neg_half", [P, NT], F32)
        wo_rows = sb("wo_rows", [P, ND, D], F32)
        wv_rows = sb("wv_rows", [P, ND, D], F32)
        small_rows = sb("small_rows", [ND * (COORDS + 1), P], F32)
        small_cols = sb("small_cols", [P, ND * (COORDS + 1)], F32)
        bv_wide = sb("bv_wide", [P, ND, P], F32)
        wo_t = sb("wo_t", [P, ND, D], F32)
        wvo = sb("wvo", [P, ND, VC], F32)
        bo_wide = sb("bo_wide", [P, D], F32)
        v_bias = sb("v_bias", [P, D], F32)
        b3d_wide = sb("b3d_wide", [P, COORDS], F32)
        scales = sb("scales", [P, 3], F32)
        signs = sb("signs", [P, 2], F32)
        magnitudes = sb("magnitudes", [P, 2], F32)
        w_factors = sb("w_factors", [P, 3], F32)
        out_factor = sb("out_factor", [P, 2], F32)
        k0_bits = sb("k0_bits", [P, 2 * ND, FF], U8)
        k1_bits = sb("k1_bits", [P, NF, FF], U8)
        k2_bits = sb("k2_bits", [P, NF, D], U8)
        w0_diff = sb("w0_diff", [P, ND, FF], F16)
        w0 = sb("w0", [P, ND, FF], F16)
        w1 = sb("w1", [P, NF, FF], F16)
        w2 = sb("w2", [P, NF, D], F16)

        x_in = sb("x_in", [P, NT, D], F32)
        x_keep = sb("x_keep", [P, NT, D], F32)
        stats1 = sb("stats1", [P, NT, 6], F32)
        mean1 = sb("mean1", [P, NT], F32)
        part1 = sb("part1", [P, 4, NT], F32)
        ve1 = sb("ve1", [P, NT], F32)
        rstd1 = sb("rstd1", [P, NT], F32)
        xn1 = sb("xn1", [P, NT, D], F32)
        xn1_t = sb("xn1_t", [P, ND, SEQ], F32)
        v = sb("v", [P, NT, D + 1], F32)
        pos = sb("pos", [P, NT, COORDS], F32)
        pos_neg = sb("pos_neg", [P, NT, COORDS], F32)
        pos_rest = sb("pos_rest", [P, 2, NT, COORDS], F32)
        pos_parts = sb("pos_parts", [P, NT, PARTS, COORDS], BF16)
        pos_t = sb("pos_t", [PARTS * COORDS, SEQ], BF16)
        square = sb("square", [P, COORDS, NS], F32)
        sum_xy = sb("sum_xy", [P, NS], F32)
        sum_xyz = sb("sum_xyz", [P, NS], F32)
        dist = sb("dist", [P, NS], F32)
        probs = sb("probs", [P, NS], F32)
        rsum = sb("rsum", [P, NT], F32)
        x1_new = sb("x1_new", [P, NT, D], F32)
        x1_cur = sb("x1_cur", [P, NT, D], F32)
        stats2 = sb("stats2", [P, NT, 6], F32)
        mean2 = sb("mean2", [P, NT], F32)
        part2 = sb("part2", [P, 4, NT], F32)
        ve2 = sb("ve2", [P, NT], F32)
        rstd2 = sb("rstd2", [P, NT], F32)
        xn2 = sb("xn2", [P, NT, D], F32)
        xn2_hi = sb("xn2_hi", [P, NT, D], F16)
        xn2_lo = sb("xn2_lo", [P, NT, D], F16)

        h_t = sb("h_t", [P, 2, ND, SEQ], F16)
        r0 = sb("r0", [P, 2, NF, SEQ], F16)
        r1 = sb("r1", [P, 2, NF, SEQ], F16)
        y = sb("y", [P, NT, D], F32)

        fbank = [psum(f"fbank{i}", [P, 512]) for i in range(FBANKS)]
        coord_bank = [psum(f"coord_bank{c}", [P, SEQ]) for c in range(COORDS)]
        mbank = [psum(f"mbank{i}", [P, 512]) for i in range(2)]

        small_loaded = sem("small_loaded")
        wo_loaded = sem("wo_loaded")
        wv_loaded = sem("wv_loaded")
        rows_loaded = sem("rows_loaded")
        scales_loaded = sem("scales_loaded")
        k0_loaded = sem("k0_loaded")
        k1_loaded = sem("k1_loaded")
        k2_loaded = sem("k2_loaded")
        filled = sem("filled")
        ident_made = sem("ident_made")
        consts_made = sem("consts_made")
        ones_made = sem("ones_made")
        wo_turned = sem("wo_turned")
        wo_t_made = sem("wo_t_made")
        small_turned = sem("small_turned")
        small_made = sem("small_made")
        bv_spread = sem("bv_spread")
        wvo_summed = sem("wvo_summed")
        wvo_made = sem("wvo_made")
        signs_made = sem("signs_made")
        factors_made = sem("factors_made")
        out_factor_made = sem("out_factor_made")
        w0_diffed = sem("w0_diffed")
        w0_made = sem("w0_made")
        w1_made = sem("w1_made")
        w2_made = sem("w2_made")
        x_loaded = sem("x_loaded")
        keep_loaded = sem("keep_loaded")
        stats1_done = sem("stats1_done")
        part1_done = sem("part1_done")
        ve1_done = sem("ve1_done")
        rstd1_done = sem("rstd1_done")
        xn1_done = sem("xn1_done")
        xn1_turned = sem("xn1_turned")
        xn1_t_even = sem("xn1_t_even")
        xn1_t_odd = sem("xn1_t_odd")
        v_summed = sem("v_summed")
        v_done = sem("v_done")
        pos_done = sem("pos_done")
        pos_neg_done = sem("pos_neg_done")
        split_done = sem("split_done")
        pos_turned = sem("pos_turned")
        pos_t_done = sem("pos_t_done")
        coords_spread = sem("coords_spread")
        squares_done = sem("squares_done")
        sum_xy_done = sem("sum_xy_done")
        sum_xyz_done = sem("sum_xyz_done")
        dist_done = sem("dist_done")
        exp_done = sem("exp_done")
        masked = sem("masked")
        attn_summed = sem("attn_summed")
        rsum_done = sem("rsum_done")
        x1_done = sem("x1_done")
        x1_moved = sem("x1_moved")
        stats2_done = sem("stats2_done")
        part2_done = sem("part2_done")
        ve2_done = sem("ve2_done")
        rstd2_done = sem("rstd2_done")
        xn2_done = sem("xn2_done")
        hi_done = sem("hi_done")
        lo_done = sem("lo_done")
        xn2_turned = sem("xn2_turned")
        h_hi_done = sem("h_hi_done")
        h_lo_done = sem("h_lo_done")
        bank_summed = sem("bank_summed")
        relu_hi_done = sem("relu_hi_done")
        bank_free = sem("bank_free")
        y_stored = sem("y_stored")

        block = ctx.enter_context(nc.Block())

        def tokens(dram, i):
            return dram[i].rearrange("(t p) d -> p t d", p=P)

        def spread(vector):
            return vector.rearrange("(a n) -> a n", a=1).to_broadcast([P, vector.shape[0]])

        @block.sync
        def _(sp):
            def load_x(i):
                if not (isinstance(i, int) and i == 0):
                    sp.wait_ge(xn1_done, i * NT)
                sp.dma_start(x_in[:, :, :], tokens(x, i)).then_inc(x_loaded, 16)

            def load_keep(i):
                if not (isinstance(i, int) and i == 0):
                    sp.wait_ge(x1_done, i * NT)
                sp.dma_start(x_keep[:, :, :], tokens(x, i)).then_inc(keep_loaded, 16)

            def move_x1(i):
                sp.dma_start(x1_cur[:, :, :], x1_new[:, :, :]).then_inc(x1_moved, 16)

            def store_y(n):
                sp.wait_ge(bank_free, n * USES + USES + FBANKS)
                sp.dma_start(tokens(out, n), y[:, :, :]).then_inc(y_stored, 16)

            load_x(0)
            sp.dma_start(wo_rows[:, :, :], wo.rearrange("(c p) d -> p c d", p=P)).then_inc(wo_loaded, 16)
            sp.dma_start(wv_rows[:, :, :], wv.rearrange("(c p) d -> p c d", p=P)).then_inc(wv_loaded, 16)
            sp.dma_start(k1_bits[:, :, :], k1.rearrange("(c p) f -> p c f", p=P)).then_inc(k1_loaded, 16)
            sp.dma_start(k0_bits[:, :, :], k0.rearrange("(c p) f -> p c f", p=P)).then_inc(k0_loaded, 16)
            sp.dma_start(k2_bits[:, :, :], k2.rearrange("(c p) f -> p c f", p=P)).then_inc(k2_loaded, 16)
            load_keep(0)
            load_x(1)
            load_keep(1)
            move_x1(0)
            load_x(2)

            def body(n, keep, ahead):
                if ahead:
                    load_x(n + 3)
                if keep:
                    load_keep(n + 2)
                store_y(n)
                sp.wait_ge(y_stored, n * 16 + 16)
                sp.wait_ge(x1_done, n * NT + 2 * NT)
                move_x1(n + 1)

            with sp.Fori(0, BATCHES - 3) as n:
                body(n, True, True)
            body(BATCHES - 3, True, False)
            body(BATCHES - 2, False, False)
            store_y(BATCHES - 1)
            sp.wait_ge(y_stored, BATCHES * 16)

        @block.gpsimd
        def _(pool):
            def rstd1_of(i):
                pool.wait_ge(ve1_done, i * 1 + 1)
                nc.gpsimd.tensor_tensor(rstd1[:, :], ve1[:, :], neg_half[:, :], ALU.pow).then_inc(rstd1_done, 1)

            def rstd2_of(i):
                pool.wait_ge(ve2_done, i * 1 + 1)
                nc.gpsimd.tensor_tensor(rstd2[:, :], ve2[:, :], neg_half[:, :], ALU.pow).then_inc(rstd2_done, 1)

            def mask(i):
                for kt in range(NT):
                    pool.wait_ge(exp_done, i * 2 + (1 if kt == 0 else 2))
                    diagonal = probs[:, ROW[kt]:ROW[kt] + P]
                    nc.gpsimd.tensor_tensor(diagonal, diagonal, causal[:, :], ALU.mult).then_inc(masked, 1)

            def low_part(i):
                for t in range(NT):
                    pool.wait_ge(hi_done, i * NT + t + 1)
                    nc.gpsimd.tensor_tensor(xn2_lo[:, t, :], xn2[:, t, :], xn2_hi[:, t, :],
                                            ALU.subtract).then_inc(lo_done, 1)

            nc.gpsimd.memset(ident[:, :], 0.0).then_inc(filled, 1)
            nc.gpsimd.memset(neg_half[:, :], -0.5).then_inc(filled, 1)
            nc.gpsimd.memset(causal[:, :], 1.0).then_inc(filled, 1)
            nc.gpsimd.memset(pick[:, :, :], 0.0).then_inc(filled, 1)
            pool.wait_ge(filled, 1)
            nc.gpsimd.affine_select(out=ident[:, :], in_=ident[:, :], compare_op=ALU.not_equal, fill=1.0, base=0,
                                    pattern=[[-1, P]], channel_multiplier=1).then_inc(ident_made, 1)
            pool.wait_ge(ident_made, 1)
            nc.gpsimd.tensor_copy(identb[:, :], ident[:, :]).then_inc(ident_made, 1)
            nc.gpsimd.tensor_copy(ident16[:, :], ident[:, :]).then_inc(ident_made, 1)
            rstd1_of(0)
            pool.wait_ge(filled, 4)
            nc.gpsimd.affine_select(out=causal[:, :], in_=causal[:, :], compare_op=ALU.is_ge, fill=0.0, base=0,
                                    pattern=[[1, P]], channel_multiplier=-1).then_inc(consts_made, 1)
            for part in range(PARTS):
                pool.wait_ge(consts_made, 1 + part)
                nc.gpsimd.affine_select(out=pick[:, :, :], in_=pick[:, :, :], compare_op=ALU.not_equal, fill=1.0,
                                        base=-COORDS * part, pattern=[[-1, COORDS], [0, P]],
                                        channel_multiplier=1).then_inc(consts_made, 1)
            pool.wait_ge(k1_loaded, 16)
            pool.wait_ge(factors_made, 3)
            for c in range(NF // 2):
                nc.gpsimd.tensor_scalar(w1[:, c, :], k1_bits[:, c, :], w_factors[:, 1:2], w_factors[:, 2:3],
                                        ALU.mult, ALU.add).then_inc(w1_made, 1)
            mask(0)
            rstd1_of(1)
            rstd2_of(0)
            low_part(0)
            pool.wait_ge(k2_loaded, 16)
            nc.gpsimd.tensor_scalar(w2[:, :, :], k2_bits[:, :, :], 2.0, -1.0, ALU.mult, ALU.add).then_inc(w2_made, 1)

            def body(n, ahead):
                if ahead:
                    rstd1_of(n + 2)
                mask(n + 1)
                rstd2_of(n + 1)
                low_part(n + 1)

            with pool.Fori(0, BATCHES - 2) as n:
                body(n, True)
            body(BATCHES - 2, False)

        @block.scalar
        def _(act):
            def turn_even(i):
                act.wait_ge(xn1_turned, i * ND + 1)
                if not (isinstance(i, int) and i == 0):
                    act.wait_ge(v_summed, i * NT)
                nc.scalar.activation(xn1_t[:, 0, :], mbank[0][:, :], ACT.Copy).then_inc(xn1_t_even, 1)

            def pos_t_out(i):
                act.wait_ge(pos_turned, i * 1 + 1)
                if not (isinstance(i, int) and i == 0):
                    act.wait_ge(coords_spread, i * 1)
                pt = mbank[0][0:PARTS * COORDS, 0:SEQ // 2].bitcast(BF16)
                nc.scalar.activation(pos_t[:, :], pt, ACT.Copy).then_inc(pos_t_done, 1)

            def squares(i, kt):
                if kt == 0:
                    act.wait_ge(coords_spread, i * 1 + 1)
                    act.wait_ge(pos_neg_done, i * 1 + 1)
                    if not (isinstance(i, int) and i == 0):
                        act.wait_ge(sum_xyz_done, i * 2)
                n = SEQ - kt * P
                for c in range(COORDS):
                    last = nc.scalar.activation(square[:, c, ROW[kt]:ROW[kt] + n], coord_bank[c][:, kt * P:SEQ],
                                                ACT.Square, bias=pos_neg[:, kt, c:c + 1])
                last.then_inc(squares_done, 1)

            def distance(i, h):
                act.wait_ge(sum_xyz_done, i * 2 + h + 1)
                a, b = CHUNKS[h]
                nc.scalar.activation(dist[:, a:b], sum_xyz[:, a:b], ACT.Sqrt).then_inc(dist_done, 1)

            def exponent(i, h):
                act.wait_ge(dist_done, i * 2 + h + 1)
                if h == 0 and not (isinstance(i, int) and i == 0):
                    act.wait_ge(attn_summed, i * NT)
                a, b = CHUNKS[h]
                nc.scalar.activation(probs[:, a:b], dist[:, a:b], ACT.Exp, scale=-SCORE_SCALE).then_inc(exp_done, 1)

            def high_part(i):
                for t in range(NT):
                    act.wait_ge(xn2_done, i * NT + t + 1)
                    if t == 0 and not (isinstance(i, int) and i == 0):
                        act.wait_ge(xn2_turned, i * 2)
                    nc.scalar.activation(xn2_hi[:, t, :], xn2[:, t, :], ACT.Copy).then_inc(hi_done, 1)

            def h_hi_out(i):
                act.wait_ge(xn2_turned, i * 2 + 1)
                nc.scalar.activation(h_t[:, 0, :, :], mbank[0][:, :].bitcast(F16), ACT.Copy).then_inc(h_hi_done, 1)

            def relu_hi(n, use):
                act.wait_ge(bank_summed, n * USES + use + 1)
                r = r0 if use < NF else r1
                nc.scalar.activation(r[:, 0, use % NF, :], fbank[use % FBANKS][:, :], ACT.Relu)\
                    .then_inc(relu_hi_done, 1)

            act.dma_start(small_rows[0:COORDS, :], w3d[:, 0:P]).then_inc(small_loaded, 16)
            act.dma_start(small_rows[COORDS:2 * COORDS, :], w3d[:, P:D]).then_inc(small_loaded, 16)
            act.dma_start(small_rows[2 * COORDS:, :], bv.rearrange("(c p) -> c p", p=P)).then_inc(small_loaded, 16)
            for j, s in enumerate((s0, s1, s2)):
                act.dma_start(scales[:, j:j + 1], spread(s)).then_inc(scales_loaded, 16)
            act.dma_start(bo_wide[:, :], spread(bo)).then_inc(rows_loaded, 16)
            act.dma_start(b3d_wide[:, :], spread(b3d)).then_inc(rows_loaded, 16)

            for c in range(ND):
                act.wait_ge(wo_turned, c + 1)
                nc.scalar.activation(wo_t[:, c, :], mbank[c][:, 0:D], ACT.Copy).then_inc(wo_t_made, 1)
            turn_even(0)
            act.wait_ge(k1_loaded, 16)
            act.wait_ge(factors_made, 3)
            for c in range(NF // 2, NF):
                nc.scalar.activation(w1[:, c, :], k1_bits[:, c, :], ACT.Identity, bias=w_factors[:, 2:3],
                                     scale=w_factors[:, 1:2]).then_inc(w1_made, 1)
            pos_t_out(0)
            for kt in range(NT):
                squares(0, kt)
            for h in range(2):
                distance(0, h)
            for h in range(2):
                exponent(0, h)
            high_part(0)
            turn_even(1)
            h_hi_out(0)

            def body(n, attention, ahead):
                relu_hi(n, 0)
                relu_hi(n, 1)
                if attention:
                    pos_t_out(n + 1)
                for m in range(2, NF):
                    relu_hi(n, m)
                if attention:
                    squares(n + 1, 0)
                relu_hi(n, NF)
                if attention:
                    squares(n + 1, 1)
                    squares(n + 1, 2)
                relu_hi(n, NF + 1)
                if attention:
                    squares(n + 1, 3)
                    distance(n + 1, 0)
                relu_hi(n, NF + 2)
                if attention:
                    distance(n + 1, 1)
                    exponent(n + 1, 0)
                relu_hi(n, NF + 3)
                if attention:
                    exponent(n + 1, 1)
                relu_hi(n, NF + 4)
                relu_hi(n, NF + 5)
                relu_hi(n, NF + 6)
                if attention:
                    high_part(n + 1)
                if ahead:
                    turn_even(n + 2)
                relu_hi(n, NF + 7)
                if attention:
                    h_hi_out(n + 1)

            with act.Fori(0, BATCHES - 2) as n:
                body(n, True, True)
            body(BATCHES - 2, True, False)
            body(BATCHES - 1, False, False)

        @block.vector
        def _(dve):
            def moments(i, stats, stats_done, mean, ve, part, part_done, scale, ve_done):
                dve.wait_ge(stats_done, i * NT + NT)
                nc.vector.tensor_tensor(part[:, 0, :], stats[:, :, 1], stats[:, :, 4], ALU.add).then_inc(part_done, 1)
                nc.vector.tensor_tensor(part[:, 1, :], stats[:, :, 1], stats[:, :, 4], ALU.subtract)\
                    .then_inc(part_done, 1)
                nc.vector.scalar_tensor_tensor(out=part[:, 2, :], in0=stats[:, :, 2], scalar=D * EPS,
                                               in1=stats[:, :, 5], op0=ALU.add, op1=ALU.add).then_inc(part_done, 1)
                dve.wait_ge(part_done, i * 5 + 2)
                nc.vector.scalar_tensor_tensor(out=part[:, 3, :], in0=part[:, 1, :], scalar=0.25 * scale,
                                               in1=part[:, 1, :], op0=ALU.mult, op1=ALU.mult).then_inc(part_done, 1)
                nc.vector.tensor_scalar(mean[:, :], part[:, 0, :], 0.5, None, ALU.mult).then_inc(part_done, 1)
                dve.wait_ge(part_done, i * 5 + 4)
                nc.vector.scalar_tensor_tensor(out=ve[:, :], in0=part[:, 2, :], scalar=scale / D,
                                               in1=part[:, 3, :], op0=ALU.mult, op1=ALU.add).then_inc(ve_done, 1)

            def ln1(i):
                dve.wait_ge(x_loaded, i * 16 + 16)
                for t in range(NT):
                    nc.vector.bn_stats(stats1[:, t, :], x_in[:, t, :]).then_inc(stats1_done, 1)
                moments(i, stats1, stats1_done, mean1, ve1, part1, part1_done, 1.0, ve1_done)

            def normalize1(i):
                dve.wait_ge(rstd1_done, i * 1 + 1)
                dve.wait_ge(part1_done, i * 5 + 5)
                if not (isinstance(i, int) and i == 0):
                    dve.wait_ge(xn1_turned, i * ND)
                for t in range(NT):
                    nc.vector.tensor_scalar(xn1[:, t, :], x_in[:, t, :], mean1[:, t:t + 1], rstd1[:, t:t + 1],
                                            ALU.subtract, ALU.mult).then_inc(xn1_done, 1)

            def turn_odd(i):
                dve.wait_ge(xn1_turned, i * ND + 2)
                if not (isinstance(i, int) and i == 0):
                    dve.wait_ge(v_summed, i * NT)
                nc.vector.tensor_copy(xn1_t[:, 1, :], mbank[1][:, :]).then_inc(xn1_t_odd, 1)

            def v_out(i, t):
                dve.wait_ge(v_summed, i * NT + t + 1)
                if t == 0 and not (isinstance(i, int) and i == 0):
                    dve.wait_ge(attn_summed, i * NT)
                    dve.wait_ge(squares_done, i * NT)
                nc.vector.tensor_tensor(pos[:, t, :], mbank[t % 2][:, D:VC], b3d_wide[:, :], ALU.add)\
                    .then_inc(pos_done, 1)
                nc.vector.tensor_tensor(v[:, t, 0:D], mbank[t % 2][:, 0:D], v_bias[:, :], ALU.add)\
                    .then_inc(v_done, 1)

            def split_pos(i):
                dve.wait_ge(pos_done, i * NT + NT)
                nc.vector.tensor_scalar(pos_neg[:, :, :], pos[:, :, :], -1.0, None, ALU.mult).then_inc(pos_neg_done, 1)
                nc.vector.tensor_copy(pos_parts[:, :, 0, :], pos[:, :, :]).then_inc(split_done, 1)
                dve.wait_ge(split_done, i * 5 + 1)
                nc.vector.tensor_tensor(pos_rest[:, 0], pos[:, :, :], pos_parts[:, :, 0, :], ALU.subtract)\
                    .then_inc(split_done, 1)
                dve.wait_ge(split_done, i * 5 + 2)
                nc.vector.tensor_copy(pos_parts[:, :, 1, :], pos_rest[:, 0]).then_inc(split_done, 1)
                dve.wait_ge(split_done, i * 5 + 3)
                nc.vector.tensor_tensor(pos_rest[:, 1], pos_rest[:, 0], pos_parts[:, :, 1, :], ALU.subtract)\
                    .then_inc(split_done, 1)
                dve.wait_ge(split_done, i * 5 + 4)
                nc.vector.tensor_copy(pos_parts[:, :, 2, :], pos_rest[:, 1]).then_inc(split_done, 1)

            def sums(i, h):
                a, b = CHUNKS[h]
                dve.wait_ge(squares_done, i * NT + (1 if h == 0 else NT))
                nc.vector.scalar_tensor_tensor(out=sum_xy[:, a:b], in0=square[:, 0, a:b], scalar=TINY,
                                               in1=square[:, 1, a:b], op0=ALU.max, op1=ALU.add)\
                    .then_inc(sum_xy_done, 1)
                dve.wait_ge(sum_xy_done, i * 2 + h + 1)
                nc.vector.tensor_tensor(sum_xyz[:, a:b], sum_xy[:, a:b], square[:, 2, a:b], ALU.add)\
                    .then_inc(sum_xyz_done, 1)

            def residual(i, t):
                dve.wait_ge(attn_summed, i * NT + t + 1)
                nc.vector.reciprocal(rsum[:, t:t + 1], mbank[t % 2][:, D:D + 1]).then_inc(rsum_done, 1)
                if t == 0:
                    dve.wait_ge(keep_loaded, i * 16 + 16)
                    if not (isinstance(i, int) and i == 0):
                        dve.wait_ge(x1_moved, i * 16)
                dve.wait_ge(rsum_done, i * NT + t + 1)
                nc.vector.scalar_tensor_tensor(out=x1_new[:, t, :], in0=mbank[t % 2][:, 0:D], scalar=rsum[:, t:t + 1],
                                               in1=x_keep[:, t, :], op0=ALU.mult, op1=ALU.add).then_inc(x1_done, 1)

            def ln2_stats(i, t):
                dve.wait_ge(x1_done, i * NT + t + 1)
                nc.vector.bn_stats(stats2[:, t, :], x1_new[:, t, :]).then_inc(stats2_done, 1)

            def ln2_var(i):
                moments(i, stats2, stats2_done, mean2, ve2, part2, part2_done, XN_SCALE ** -2, ve2_done)

            def normalize2(i):
                dve.wait_ge(rstd2_done, i * 1 + 1)
                dve.wait_ge(part2_done, i * 5 + 5)
                if not (isinstance(i, int) and i == 0):
                    dve.wait_ge(lo_done, i * NT)
                for t in range(NT):
                    nc.vector.tensor_scalar(xn2[:, t, :], x1_new[:, t, :], mean2[:, t:t + 1], rstd2[:, t:t + 1],
                                            ALU.subtract, ALU.mult).then_inc(xn2_done, 1)

            def h_lo_out(i):
                dve.wait_ge(xn2_turned, i * 2 + 2)
                nc.vector.tensor_copy(h_t[:, 1, :, :], mbank[1][:, :].bitcast(F16)).then_inc(h_lo_done, 1)

            def relu_lo(n, use):
                r = r0 if use < NF else r1
                dve.wait_ge(relu_hi_done, n * 2 * NF + use + 1)
                nc.vector.scalar_tensor_tensor(out=r[:, 1, use % NF, :], in0=fbank[use % FBANKS][:, :], scalar=0.0,
                                               in1=r[:, 0, use % NF, :], op0=ALU.max, op1=ALU.subtract)\
                    .then_inc(bank_free, 1)

            def finish(n, half):
                use = 2 * NF + half
                dve.wait_ge(bank_summed, n * USES + use + 1)
                if half == 0:
                    dve.wait_ge(x1_moved, n * 16 + 16)
                t = 2 * half
                z = fbank[use % FBANKS][:, :].rearrange("p (t d) -> p t d", d=D)
                nc.vector.scalar_tensor_tensor(out=y[:, t:t + 2, :], in0=z, scalar=out_factor[:, 1:2],
                                               in1=x1_cur[:, t:t + 2, :], op0=ALU.mult, op1=ALU.add)\
                    .then_inc(bank_free, 1)

            ln1(0)
            nc.vector.memset(v[:, :, D:D + 1], 1.0).then_inc(bank_free, FBANKS)
            dve.wait_ge(small_turned, 1)
            nc.vector.tensor_copy(small_cols[:, :], fbank[0][:, 0:ND * (COORDS + 1)]).then_inc(small_made, 1)
            dve.wait_ge(small_made, 1)
            for c in range(ND):
                nc.vector.tensor_copy(wvo[:, c, D:VC], small_cols[:, c * COORDS:(c + 1) * COORDS])
                j = ND * COORDS + c
                nc.vector.tensor_copy(bv_wide[:, c, :], small_cols[:, j:j + 1].to_broadcast([P, P]))\
                    .then_inc(bv_spread, 1)
            normalize1(0)
            for c in range(ND):
                dve.wait_ge(wvo_summed, c + 1)
                nc.vector.tensor_copy(wvo[:, c, 0:D], fbank[1 + c][:, 0:D]).then_inc(wvo_made, 1)
            turn_odd(0)
            dve.wait_ge(wvo_summed, ND + 1)
            dve.wait_ge(rows_loaded, 32)
            nc.vector.tensor_tensor(v_bias[:, :], fbank[0][:, 0:D], bo_wide[:, :], ALU.add).then_inc(wvo_made, 1)
            dve.wait_ge(scales_loaded, 48)
            nc.vector.tensor_scalar(signs[:, :], scales[:, 0:2], 0.0, 2.0, ALU.is_ge, ALU.mult).then_inc(signs_made, 1)
            dve.wait_ge(signs_made, 1)
            nc.vector.tensor_scalar(signs[:, :], signs[:, :], -1.0, None, ALU.add).then_inc(signs_made, 1)
            dve.wait_ge(signs_made, 2)
            nc.vector.tensor_tensor(magnitudes[:, :], scales[:, 0:2], signs[:, :], ALU.mult).then_inc(signs_made, 1)
            nc.vector.tensor_scalar(w_factors[:, 0:1], signs[:, 0:1], 2.0 * W0_SCALE, None, ALU.mult)\
                .then_inc(factors_made, 1)
            nc.vector.tensor_scalar(w_factors[:, 1:2], signs[:, 1:2], 2.0 * W1_SCALE, None, ALU.mult)\
                .then_inc(factors_made, 1)
            nc.vector.tensor_scalar(w_factors[:, 2:3], signs[:, 1:2], -W1_SCALE, None, ALU.mult)\
                .then_inc(factors_made, 1)
            dve.wait_ge(wvo_made, ND + 1)
            for t in range(NT):
                v_out(0, t)
            split_pos(0)
            dve.wait_ge(k0_loaded, 16)
            nc.vector.tensor_tensor(w0_diff[:, :, :], k0_bits[:, 0:ND, :], k0_bits[:, ND:2 * ND, :], ALU.subtract)\
                .then_inc(w0_diffed, 1)
            dve.wait_ge(w0_diffed, 1)
            dve.wait_ge(factors_made, 3)
            nc.vector.tensor_scalar(w0[:, :, :], w0_diff[:, :, :], w_factors[:, 0:1], None, ALU.mult)\
                .then_inc(w0_made, 1)
            dve.wait_ge(signs_made, 3)
            nc.vector.scalar_tensor_tensor(out=out_factor[:, 0:1], in0=magnitudes[:, 0:1], scalar=OUT_SCALE,
                                           in1=magnitudes[:, 1:2], op0=ALU.mult, op1=ALU.mult)\
                .then_inc(out_factor_made, 1)
            dve.wait_ge(out_factor_made, 1)
            nc.vector.tensor_tensor(out_factor[:, 1:2], out_factor[:, 0:1], scales[:, 2:3], ALU.mult)\
                .then_inc(out_factor_made, 1)
            sums(0, 0)
            sums(0, 1)
            ln1(1)
            normalize1(1)
            for t in range(NT):
                residual(0, t)
                ln2_stats(0, t)
            ln2_var(0)
            turn_odd(1)
            normalize2(0)
            h_lo_out(0)
            for t in range(NT):
                v_out(1, t)
            split_pos(1)
            dve.wait_ge(out_factor_made, 2)

            def body(n, attention, ahead):
                for m in range(NF + 1):
                    relu_lo(n, m)
                if attention:
                    sums(n + 1, 0)
                if ahead:
                    ln1(n + 2)
                relu_lo(n, NF + 1)
                if attention:
                    sums(n + 1, 1)
                relu_lo(n, NF + 2)
                if ahead:
                    normalize1(n + 2)
                relu_lo(n, NF + 3)
                relu_lo(n, NF + 4)
                if attention:
                    for t in range(NT):
                        residual(n + 1, t)
                    relu_lo(n, NF + 5)
                    for t in range(NT):
                        ln2_stats(n + 1, t)
                    ln2_var(n + 1)
                    relu_lo(n, NF + 6)
                    if ahead:
                        turn_odd(n + 2)
                    normalize2(n + 1)
                else:
                    relu_lo(n, NF + 5)
                    relu_lo(n, NF + 6)
                relu_lo(n, NF + 7)
                if attention:
                    h_lo_out(n + 1)
                finish(n, 0)
                if ahead:
                    for t in range(NT):
                        v_out(n + 2, t)
                    split_pos(n + 2)
                finish(n, 1)

            with dve.Fori(0, BATCHES - 2) as n:
                body(n, True, True)
            body(BATCHES - 2, True, False)
            body(BATCHES - 1, False, False)

        @block.tensor
        def _(pe):
            def turn_xn1(i):
                pe.wait_ge(xn1_done, i * NT + NT)
                for c in range(ND):
                    for t in range(NT):
                        last = nc.tensor.transpose(mbank[c][:, t * P:(t + 1) * P], xn1[:, t, c * P:(c + 1) * P],
                                                   ident[:, :])
                    last.then_inc(xn1_turned, 1)

            def values(i, t):
                if t == 0:
                    pe.wait_ge(xn1_t_even, i * 1 + 1)
                    pe.wait_ge(xn1_t_odd, i * 1 + 1)
                if t >= 2:
                    pe.wait_ge(v_done, i * NT + t - 1)
                for c in range(ND):
                    last = nc.tensor.matmul(mbank[t % 2][:, 0:VC], xn1_t[:, c, t * P:(t + 1) * P], wvo[:, c, :],
                                            start=(c == 0), stop=(c == ND - 1))
                last.then_inc(v_summed, 1)

            def turn_pos(i):
                pe.wait_ge(split_done, i * 5 + 5)
                pe.wait_ge(v_done, i * NT + NT)
                pt = mbank[0][0:PARTS * COORDS, 0:SEQ // 2].bitcast(BF16)
                for t in range(NT):
                    last = nc.tensor.transpose(pt[:, t * P:(t + 1) * P],
                                               pos_parts[:, t].rearrange("p a c -> p (a c)"), identb[:, :])
                last.then_inc(pos_turned, 1)

            def spread_coords(i):
                pe.wait_ge(pos_t_done, i * 1 + 1)
                if not (isinstance(i, int) and i == 0):
                    pe.wait_ge(squares_done, i * NT)
                for c in range(COORDS):
                    last = nc.tensor.matmul(coord_bank[c][:, :], pick[:, c, :], pos_t[:, :], start=True, stop=True)
                last.then_inc(coords_spread, 1)

            def attend(i, qt):
                pe.wait_ge(masked, i * NT + qt + 1)
                if qt == 0:
                    pe.wait_ge(pos_t_done, i * 1 + 1)
                if qt >= 2:
                    pe.wait_ge(x1_done, i * NT + qt - 1)
                for kt in range(qt + 1):
                    col = ROW[kt] + (qt - kt) * P
                    last = nc.tensor.matmul(mbank[qt % 2][:, 0:D + 1], probs[:, col:col + P], v[:, kt, :],
                                            start=(kt == 0), stop=(kt == qt))
                last.then_inc(attn_summed, 1)

            def turn_xn2(i):
                for part, source, done in ((0, xn2_hi, hi_done), (1, xn2_lo, lo_done)):
                    pe.wait_ge(done, i * NT + NT)
                    turned = mbank[part][:, :].bitcast(F16)
                    for c in range(ND):
                        for t in range(NT):
                            at = c * SEQ + t * P
                            last = nc.tensor.transpose(turned[:, at:at + P], source[:, t, c * P:(c + 1) * P],
                                                       ident16[:, :])
                    last.then_inc(xn2_turned, 1)

            def hidden(n, use, weights, source, k_tiles):
                pe.wait_ge(bank_free, n * USES + use + 1)
                m = use % NF
                for k in range(k_tiles):
                    for part in range(2):
                        last = nc.tensor.matmul(fbank[use % FBANKS][:, :], weights[:, k, m * P:(m + 1) * P],
                                                source[:, part, k, :], start=(k == 0 and part == 0),
                                                stop=(k == k_tiles - 1 and part == 1))
                last.then_inc(bank_summed, 1)

            def layer0(n, m):
                if m == 0:
                    pe.wait_ge(h_hi_done, n * 1 + 1)
                    pe.wait_ge(h_lo_done, n * 1 + 1)
                hidden(n, m, w0, h_t, ND)

            def layer1(n, m):
                if m == 0:
                    pe.wait_ge(bank_free, n * USES + NF + FBANKS)
                hidden(n, NF + m, w1, r0, NF)

            def layer2(n, half):
                use = 2 * NF + half
                if half == 0:
                    pe.wait_ge(bank_free, n * USES + 2 * NF + FBANKS)
                else:
                    pe.wait_ge(bank_free, n * USES + use + 1)
                for s in range(2):
                    t = 2 * half + s
                    for k in range(NF):
                        for part in range(2):
                            last = nc.tensor.matmul(fbank[use % FBANKS][:, s * D:(s + 1) * D],
                                                    r1[:, part, k, t * P:(t + 1) * P], w2[:, k, :],
                                                    start=(k == 0 and part == 0), stop=(k == NF - 1 and part == 1))
                last.then_inc(bank_summed, 1)

            pe.wait_ge(ident_made, 1)
            pe.wait_ge(small_loaded, 48)
            nc.tensor.transpose(fbank[0][:, 0:ND * (COORDS + 1)], small_rows[:, :],
                                ident[0:ND * (COORDS + 1), 0:ND * (COORDS + 1)]).then_inc(small_turned, 1)
            pe.wait_ge(wo_loaded, 16)
            for c in range(ND):
                for o in range(ND):
                    last = nc.tensor.transpose(mbank[c][:, o * P:(o + 1) * P], wo_rows[:, o, c * P:(c + 1) * P],
                                               ident[:, :])
                last.then_inc(wo_turned, 1)
            pe.wait_ge(wv_loaded, 16)
            pe.wait_ge(wo_t_made, ND)
            for c in range(ND):
                for j in range(ND):
                    last = nc.tensor.matmul(fbank[1 + c][:, 0:D], wv_rows[:, j, c * P:(c + 1) * P], wo_t[:, j, :],
                                            start=(j == 0), stop=(j == ND - 1))
                last.then_inc(wvo_summed, 1)
            turn_xn1(0)
            pe.wait_ge(bv_spread, ND)
            for j in range(ND):
                last = nc.tensor.matmul(fbank[0][:, 0:D], bv_wide[:, j, :], wo_t[:, j, :],
                                        start=(j == 0), stop=(j == ND - 1))
            last.then_inc(wvo_summed, 1)
            pe.wait_ge(wvo_made, ND)
            for t in range(NT):
                values(0, t)
            pe.wait_ge(ident_made, 3)
            turn_pos(0)
            pe.wait_ge(consts_made, 1 + PARTS)
            spread_coords(0)
            for qt in range(NT):
                attend(0, qt)
            pe.wait_ge(x1_done, NT)
            turn_xn1(1)
            pe.wait_ge(xn1_t_even, 2)
            pe.wait_ge(xn1_t_odd, 2)
            turn_xn2(0)
            pe.wait_ge(h_hi_done, 1)
            pe.wait_ge(h_lo_done, 1)
            for t in range(NT):
                values(1, t)
            pe.wait_ge(w0_made, 1)
            pe.wait_ge(w1_made, NF)
            pe.wait_ge(w2_made, 1)

            def body(n, attention, ahead):
                layer0(n, 0)
                if attention:
                    turn_pos(n + 1)
                layer0(n, 1)
                layer0(n, 2)
                if attention:
                    spread_coords(n + 1)
                for m in range(3, NF):
                    layer0(n, m)
                for m in range(0, 6):
                    layer1(n, m)
                if attention:
                    for qt in range(NT):
                        attend(n + 1, qt)
                layer1(n, 6)
                if ahead:
                    pe.wait_ge(x1_done, n * NT + 2 * NT)
                    turn_xn1(n + 2)
                layer1(n, 7)
                if attention:
                    if ahead:
                        pe.wait_ge(xn1_t_even, n * 1 + 3)
                        pe.wait_ge(xn1_t_odd, n * 1 + 3)
                    turn_xn2(n + 1)
                layer2(n, 0)
                if ahead:
                    pe.wait_ge(h_hi_done, n * 1 + 2)
                    pe.wait_ge(h_lo_done, n * 1 + 2)
                    for t in range(NT):
                        values(n + 2, t)
                layer2(n, 1)

            with pe.Fori(0, BATCHES - 2) as n:
                body(n, True, True)
            body(BATCHES - 2, True, False)
            body(BATCHES - 1, False, False)


INPUTS = ["L0_attn_x", "L0_attn_wv", "L0_attn_bv", "L0_attn_wo", "L0_attn_bo", "L0_attn_w3d", "L0_attn_b3d",
          "L0_ffn_k0", "L0_ffn_k1", "L0_ffn_k2", "L0_ffn_s0", "L0_ffn_s1", "L0_ffn_s2"]


def kernel(**inputs):
    import numpy as np
    import concourse.bacc as bacc
    from concourse.bass_utils import run_bass_kernel_spmd

    nc = bacc.Bacc("TRN2", target_bir_lowering=False, num_devices=1)
    arrays, args = {}, []
    for name in INPUTS:
        a = np.ascontiguousarray(inputs[name])
        if a.ndim == 0:
            a = a.reshape(1)
        arrays[name + "_dram"] = a
        args.append(nc.dram_tensor(name + "_dram", a.shape, mybir.dt.from_np(a.dtype), kind="ExternalInput").ap())
    shape = inputs["L0_attn_x"].shape
    args.append(nc.dram_tensor("out_dram", shape, F32, kind="ExternalOutput").ap())
    block_kernel(nc, *args)
    result = run_bass_kernel_spmd(nc, [arrays], core_ids=[0])
    return result.results[0]["out_dram"]
```

```python
from contextlib import ExitStack

import concourse.bass as bass
from concourse import mybir

ALU = mybir.AluOpType
ACT = mybir.ActivationFunctionType
F32 = mybir.dt.float32
F16 = mybir.dt.float16
BF16 = mybir.dt.bfloat16
U8 = mybir.dt.uint8
I32 = mybir.dt.int32
AX_X = mybir.AxisListType.X

P = 128
HEADS = 16
EPS = 1e-5
TINY = 2.0 ** -100
XN_SCALE = 2.0 ** 10
W0_SCALE = 2.0 ** -4
W1_SCALE = 2.0 ** -10
OUT_SCALE = 2.0 ** 4 * 4.0
W_SCALE = 2.0 ** 14
V_SCALE = 2.0 ** 6
E_SCALE = 2.0 ** 15
FBANKS = 3


def block_kernel(nc, x, wv, bv, wo, bo, w3d, b3d, k0, k1, k2, s0, s1, s2, out):
    BATCHES, SEQ, D = x.shape
    FF = k1.shape[0]
    NT = SEQ // P
    ND = D // P
    NF = FF // P
    COORDS = w3d.shape[0]
    PARTS = 3
    SCORE_SCALE = 1.0 / (D // HEADS) ** 0.5
    USES = 2 * NF + NT // 2
    VC = D + COORDS
    ROW = [sum(SEQ - j * P for j in range(kt)) for kt in range(NT)]
    NS = ROW[-1] + SEQ - (NT - 1) * P
    NS_OPS = NT * COORDS
    W1_ON_POOL = NF - 2
    KEY_ORDER = [*range(1, NT), 0]
    CHUNKS = [(SEQ, NS), (0, SEQ)]
    assert USES % FBANKS == 0 and FF == k0.shape[1] and k0.shape[0] == 2 * D

    with ExitStack() as ctx:
        def sb(name, shape, dt):
            return ctx.enter_context(nc.sbuf_tensor(name, shape, dt))

        def psum(name, shape, dt=F32):
            return ctx.enter_context(nc.psum_tensor(name, shape, dt))

        def sem(name):
            return ctx.enter_context(nc.semaphore(name))

        ident = sb("ident", [P, P], F32)
        ident16 = sb("ident16", [P, P], F16)
        identb = sb("identb", [P, P], BF16)
        causal = sb("causal", [P, P], F32)
        pick = sb("pick", [PARTS * COORDS, COORDS, P], BF16)
        neg_half = sb("neg_half", [P, NT], F32)
        wo_rows = sb("wo_rows", [P, ND, D], F32)
        wv_rows = sb("wv_rows", [P, ND, D], F32)
        small_rows = sb("small_rows", [ND * (COORDS + 1), P], F32)
        small_cols = sb("small_cols", [P, ND * (COORDS + 1)], F32)
        largest_of_tile = sb("largest_of_tile", [P, ND], F32)
        ones_row = sb("ones_row", [1, P], F32)
        largest = sb("largest", [P, 2], F32)
        largest_row = sb("largest_row", [1, 2], F32)
        powers = sb("powers", [1, 2, 2], F32)
        factors = sb("factors", [P, 2, 2], F32)
        bv_wide = sb("bv_wide", [P, ND, P], F32)
        wo_t = sb("wo_t", [P, ND, D], F32)
        wvo = sb("wvo", [P, 2, ND, VC], F16)
        bo_wide = sb("bo_wide", [P, D], F32)
        v_bias = sb("v_bias", [P, D], F32)
        b3d_wide = sb("b3d_wide", [P, COORDS], F32)
        scales = sb("scales", [P, 3], F32)
        signs = sb("signs", [P, 2], F32)
        magnitudes = sb("magnitudes", [P, 2], F32)
        w_factors = sb("w_factors", [P, 3], F32)
        out_factor = sb("out_factor", [P, 2], F32)
        k0_bits = sb("k0_bits", [P, 2 * ND, FF], U8)
        k1_bits = sb("k1_bits", [P, NF, FF], U8)
        k2_bits = sb("k2_bits", [P, NF, D], U8)
        w0_diff = sb("w0_diff", [P, ND, FF], F16)
        w0 = sb("w0", [P, ND, FF], F16)
        w1 = sb("w1", [P, NF, FF], F16)
        w2 = sb("w2", [P, NF, D], F16)

        x_in = sb("x_in", [P, NT, D], F32)
        x_keep = sb("x_keep", [P, NT, D], F32)
        stats1 = sb("stats1", [P, NT, 6], F32)
        mean1 = sb("mean1", [P, NT], F32)
        part1 = sb("part1", [P, 4, NT], F32)
        ve1 = sb("ve1", [P, NT], F32)
        rstd1 = sb("rstd1", [P, NT], F32)
        xn1 = sb("xn1", [P, NT, D], F32)
        xn1_t = sb("xn1_t", [P, 2, ND, SEQ], F16)
        v = sb("v", [P, 2, NT, D + 1], F16)
        pos = sb("pos", [P, NT, COORDS], F32)
        pos_neg = sb("pos_neg", [P, NT, COORDS], F32)
        pos_rest = sb("pos_rest", [P, 2, NT, COORDS], F32)
        pos_parts = sb("pos_parts", [P, NT, PARTS, COORDS], BF16)
        pos_t = sb("pos_t", [PARTS * COORDS, SEQ], BF16)
        square = sb("square", [P, COORDS, NS], F32)
        sum_xy = sb("sum_xy", [P, NS], F32)
        sum_xyz = sb("sum_xyz", [P, NS], F32)
        dist = sb("dist", [P, NS], F32)
        probs = sb("probs", [P, NS], F32)
        probs_hi = sb("probs_hi", [P, NS], F16)
        probs_lo = sb("probs_lo", [P, NS], F16)
        rsum = sb("rsum", [P, 2, NT], F32)
        x_biased = sb("x_biased", [P, NT, D], F32)
        x1_new = sb("x1_new", [P, NT, D], F32)
        x1_cur = sb("x1_cur", [P, NT, D], F32)
        stats2 = sb("stats2", [P, NT, 6], F32)
        mean2 = sb("mean2", [P, NT], F32)
        part2 = sb("part2", [P, 4, NT], F32)
        ve2 = sb("ve2", [P, NT], F32)
        rstd2 = sb("rstd2", [P, NT], F32)
        xn2 = sb("xn2", [P, NT, D], F32)
        xn2_hi = sb("xn2_hi", [P, NT, D], F16)
        xn2_lo = sb("xn2_lo", [P, NT, D], F16)

        h_t = sb("h_t", [P, 2, ND, SEQ], F16)
        r0 = sb("r0", [P, 2, NF, SEQ], F16)
        r1 = sb("r1", [P, 2, NF, SEQ], F16)
        y = sb("y", [P, NT, D], F32)

        fbank = [psum(f"fbank{i}", [P, 512]) for i in range(FBANKS)]
        coord_bank = [psum(f"coord_bank{c}", [P, SEQ]) for c in range(COORDS)]
        mbank = [psum(f"mbank{i}", [P, 512]) for i in range(2)]

        small_loaded = sem("small_loaded")
        wo_loaded = sem("wo_loaded")
        wv_loaded = sem("wv_loaded")
        rows_loaded = sem("rows_loaded")
        scales_loaded = sem("scales_loaded")
        k0_loaded = sem("k0_loaded")
        k1_loaded = sem("k1_loaded")
        k2_loaded = sem("k2_loaded")
        filled = sem("filled")
        ident_made = sem("ident_made")
        consts_made = sem("consts_made")
        wo_turned = sem("wo_turned")
        wo_t_made = sem("wo_t_made")
        small_turned = sem("small_turned")
        small_made = sem("small_made")
        bv_spread = sem("bv_spread")
        wvo_summed = sem("wvo_summed")
        ones_made = sem("ones_made")
        abs_done = sem("abs_done")
        largest_found = sem("largest_found")
        largest_turned = sem("largest_turned")
        power_steps = sem("power_steps")
        powers_spread = sem("powers_spread")
        powers_known = sem("powers_known")
        weights_hi_made = sem("weights_hi_made")
        w3d_made = sem("w3d_made")
        wvo_made = sem("wvo_made")
        v_bias_made = sem("v_bias_made")
        signs_made = sem("signs_made")
        factors_made = sem("factors_made")
        out_factor_made = sem("out_factor_made")
        w0_diffed = sem("w0_diffed")
        w0_made = sem("w0_made")
        w1_made = sem("w1_made")
        w2_made = sem("w2_made")
        x_loaded = sem("x_loaded")
        keep_loaded = sem("keep_loaded")
        stats1_done = sem("stats1_done")
        part1_done = sem("part1_done")
        ve1_done = sem("ve1_done")
        rstd1_done = sem("rstd1_done")
        xn1_done = sem("xn1_done")
        xn1_turned = sem("xn1_turned")
        xn1_t_hi_done = sem("xn1_t_hi_done")
        xn1_t_done = sem("xn1_t_done")
        v_summed = sem("v_summed")
        pos_summed = sem("pos_summed")
        v_hi_done = sem("v_hi_done")
        v_done = sem("v_done")
        pos_done = sem("pos_done")
        pos_neg_done = sem("pos_neg_done")
        split_done = sem("split_done")
        pos_turned = sem("pos_turned")
        pos_t_done = sem("pos_t_done")
        coords_spread = sem("coords_spread")
        squares_done = sem("squares_done")
        sum_xy_done = sem("sum_xy_done")
        sum_xyz_done = sem("sum_xyz_done")
        dist_done = sem("dist_done")
        exp_done = sem("exp_done")
        masked = sem("masked")
        probs_hi_done = sem("probs_hi_done")
        probs_done = sem("probs_done")
        biased = sem("biased")
        attn_summed = sem("attn_summed")
        rsum_done = sem("rsum_done")
        x1_done = sem("x1_done")
        x1_moved = sem("x1_moved")
        stats2_done = sem("stats2_done")
        part2_done = sem("part2_done")
        ve2_done = sem("ve2_done")
        rstd2_done = sem("rstd2_done")
        xn2_done = sem("xn2_done")
        hi_done = sem("hi_done")
        lo_done = sem("lo_done")
        xn2_turned = sem("xn2_turned")
        h_hi_done = sem("h_hi_done")
        h_lo_done = sem("h_lo_done")
        bank_summed = sem("bank_summed")
        relu_hi_done = sem("relu_hi_done")
        bank_free = sem("bank_free")
        y_stored = sem("y_stored")

        block = ctx.enter_context(nc.Block())

        def tokens(dram, i):
            return dram[i].rearrange("(t p) d -> p t d", p=P)

        def spread(vector):
            return vector.rearrange("(a n) -> a n", a=1).to_broadcast([P, vector.shape[0]])

        @block.sync
        def _(sp):
            def load_x(i):
                if not (isinstance(i, int) and i == 0):
                    sp.wait_ge(xn1_done, i * NT)
                sp.dma_start(x_in[:, :, :], tokens(x, i)).then_inc(x_loaded, 16)

            def load_keep(i):
                if not (isinstance(i, int) and i == 0):
                    sp.wait_ge(biased, i * NT)
                sp.dma_start(x_keep[:, :, :], tokens(x, i)).then_inc(keep_loaded, 16)

            def move_x1(i):
                sp.dma_start(x1_cur[:, :, :], x1_new[:, :, :]).then_inc(x1_moved, 16)

            def store_y(n):
                for half in range(2):
                    sp.wait_ge(bank_free, n * USES + 2 * NF + half + 1 + FBANKS)
                    t = 2 * half
                    sp.dma_start(tokens(out, n)[:, t:t + 2, :], y[:, t:t + 2, :]).then_inc(y_stored, 16)

            load_x(0)
            sp.dma_start(wo_rows[:, :, :], wo.rearrange("(c p) d -> p c d", p=P)).then_inc(wo_loaded, 16)
            sp.dma_start(wv_rows[:, :, :], wv.rearrange("(c p) d -> p c d", p=P)).then_inc(wv_loaded, 16)
            sp.dma_start(k1_bits[:, :, :], k1.rearrange("(c p) f -> p c f", p=P)).then_inc(k1_loaded, 16)
            sp.dma_start(k0_bits[:, :, :], k0.rearrange("(c p) f -> p c f", p=P)).then_inc(k0_loaded, 16)
            sp.dma_start(k2_bits[:, :, :], k2.rearrange("(c p) f -> p c f", p=P)).then_inc(k2_loaded, 16)
            load_keep(0)
            load_x(1)
            load_keep(1)
            load_x(2)
            sp.wait_ge(x1_done, NT)
            move_x1(0)

            def body(n, keep, ahead):
                if ahead:
                    load_x(n + 3)
                if keep:
                    load_keep(n + 2)
                store_y(n)
                sp.wait_ge(y_stored, n * 32 + 32)
                sp.wait_ge(x1_done, n * NT + 2 * NT)
                move_x1(n + 1)

            with sp.Fori(0, BATCHES - 3) as n:
                body(n, True, True)
            body(BATCHES - 3, True, False)
            body(BATCHES - 2, False, False)
            store_y(BATCHES - 1)
            sp.wait_ge(y_stored, BATCHES * 32)

        @block.gpsimd
        def _(pool):
            def rstd1_of(i):
                pool.wait_ge(ve1_done, i * 1 + 1)
                nc.gpsimd.tensor_tensor(rstd1[:, :], ve1[:, :], neg_half[:, :], ALU.pow).then_inc(rstd1_done, 1)

            def rstd2_of(i):
                pool.wait_ge(ve2_done, i * 1 + 1)
                nc.gpsimd.tensor_tensor(rstd2[:, :], ve2[:, :], neg_half[:, :], ALU.pow).then_inc(rstd2_done, 1)

            def mask(i):
                for kt in KEY_ORDER:
                    pool.wait_ge(exp_done, i * 2 + (2 if kt == 0 else 1))
                    diagonal = probs[:, ROW[kt]:ROW[kt] + P]
                    nc.gpsimd.tensor_tensor(diagonal, diagonal, causal[:, :], ALU.mult).then_inc(masked, 1)

            def bias_x(i):
                pool.wait_ge(keep_loaded, i * 16 + 16)
                if not (isinstance(i, int) and i == 0):
                    pool.wait_ge(x1_done, i * NT)
                for t in range(NT):
                    nc.gpsimd.tensor_tensor(x_biased[:, t, :], x_keep[:, t, :], v_bias[:, :], ALU.add)\
                        .then_inc(biased, 1)

            nc.gpsimd.memset(ident[:, :], 0.0).then_inc(filled, 1)
            nc.gpsimd.memset(neg_half[:, :], -0.5).then_inc(filled, 1)
            nc.gpsimd.memset(causal[:, :], 1.0).then_inc(filled, 1)
            nc.gpsimd.memset(pick[:, :, :], 0.0).then_inc(filled, 1)
            pool.wait_ge(filled, 1)
            nc.gpsimd.affine_select(out=ident[:, :], in_=ident[:, :], compare_op=ALU.not_equal, fill=1.0, base=0,
                                    pattern=[[-1, P]], channel_multiplier=1).then_inc(ident_made, 1)
            pool.wait_ge(ident_made, 1)
            nc.gpsimd.tensor_copy(identb[:, :], ident[:, :]).then_inc(ident_made, 1)
            nc.gpsimd.tensor_copy(ident16[:, :], ident[:, :]).then_inc(ident_made, 1)
            rstd1_of(0)
            pool.wait_ge(filled, 4)
            nc.gpsimd.affine_select(out=causal[:, :], in_=causal[:, :], compare_op=ALU.is_ge, fill=0.0, base=0,
                                    pattern=[[1, P]], channel_multiplier=-1).then_inc(consts_made, 1)
            for part in range(PARTS):
                pool.wait_ge(consts_made, 1 + part)
                nc.gpsimd.affine_select(out=pick[:, :, :], in_=pick[:, :, :], compare_op=ALU.not_equal, fill=1.0,
                                        base=-COORDS * part, pattern=[[-1, COORDS], [0, P]],
                                        channel_multiplier=1).then_inc(consts_made, 1)
            pool.wait_ge(k1_loaded, 16)
            pool.wait_ge(factors_made, 3)
            for c in range(W1_ON_POOL):
                nc.gpsimd.tensor_scalar(w1[:, c, :], k1_bits[:, c, :], w_factors[:, 1:2], w_factors[:, 2:3],
                                        ALU.mult, ALU.add).then_inc(w1_made, 1)
            rstd1_of(1)
            pool.wait_ge(v_bias_made, 1)
            bias_x(0)
            mask(0)
            rstd2_of(0)
            pool.wait_ge(k2_loaded, 16)
            nc.gpsimd.tensor_scalar(w2[:, :, :], k2_bits[:, :, :], 2.0, -1.0, ALU.mult, ALU.add).then_inc(w2_made, 1)

            def body(n, ahead):
                if ahead:
                    rstd1_of(n + 2)
                mask(n + 1)
                bias_x(n + 1)
                rstd2_of(n + 1)

            with pool.Fori(0, BATCHES - 2) as n:
                body(n, True)
            body(BATCHES - 2, False)

        @block.scalar
        def _(act):
            def xn1_hi(i):
                for c in range(ND):
                    act.wait_ge(xn1_turned, i * ND + c + 1)
                    if c == 0 and not (isinstance(i, int) and i == 0):
                        act.wait_ge(v_summed, i * NT)
                    nc.scalar.activation(xn1_t[:, 0, c, :], mbank[c][:, :], ACT.Copy).then_inc(xn1_t_hi_done, 1)

            def v_hi(i, t):
                act.wait_ge(v_summed, i * NT + t + 1)
                if t == 0 and not (isinstance(i, int) and i == 0):
                    act.wait_ge(attn_summed, i * NT)
                nc.scalar.activation(v[:, 0, t, 0:D], mbank[t % 2][:, 0:D], ACT.Copy,
                                     scale=V_SCALE / (XN_SCALE * W_SCALE)).then_inc(v_hi_done, 1)

            def pos_t_out(i):
                act.wait_ge(pos_turned, i * 1 + 1)
                if not (isinstance(i, int) and i == 0):
                    act.wait_ge(coords_spread, i * 1)
                pt = mbank[0][0:PARTS * COORDS, 0:SEQ // 2].bitcast(BF16)
                nc.scalar.activation(pos_t[:, :], pt, ACT.Copy).then_inc(pos_t_done, 1)

            def squares(i, kt, coords=range(COORDS)):
                if kt == NT - 1 and 0 in coords:
                    act.wait_ge(coords_spread, i * 1 + 1)
                    act.wait_ge(pos_neg_done, i * 1 + 1)
                    if not (isinstance(i, int) and i == 0):
                        act.wait_ge(sum_xyz_done, i * 2)
                n = SEQ - kt * P
                for c in coords:
                    nc.scalar.activation(square[:, c, ROW[kt]:ROW[kt] + n], coord_bank[c][:, kt * P:SEQ],
                                         ACT.Square, bias=pos_neg[:, kt, c:c + 1]).then_inc(squares_done, 1)

            def distance(i, h):
                act.wait_ge(sum_xyz_done, i * 2 + h + 1)
                a, b = CHUNKS[h]
                nc.scalar.activation(dist[:, a:b], sum_xyz[:, a:b], ACT.Sqrt).then_inc(dist_done, 1)

            def exponent(i, h):
                act.wait_ge(dist_done, i * 2 + h + 1)
                if h == 0 and not (isinstance(i, int) and i == 0):
                    act.wait_ge(probs_done, i * NT)
                a, b = CHUNKS[h]
                nc.scalar.activation(probs[:, a:b], dist[:, a:b], ACT.Exp, scale=-SCORE_SCALE).then_inc(exp_done, 1)

            def probs_high(i):
                for j, kt in enumerate(KEY_ORDER):
                    act.wait_ge(masked, i * NT + j + 1)
                    if j == 0 and not (isinstance(i, int) and i == 0):
                        act.wait_ge(attn_summed, i * NT)
                    row = slice(ROW[kt], ROW[kt] + SEQ - kt * P)
                    nc.scalar.activation(probs_hi[:, row], probs[:, row], ACT.Copy, scale=E_SCALE)\
                        .then_inc(probs_hi_done, 1)

            def high_part(i):
                for t in range(NT):
                    act.wait_ge(xn2_done, i * NT + t + 1)
                    if t == 0 and not (isinstance(i, int) and i == 0):
                        act.wait_ge(xn2_turned, i * 2)
                    nc.scalar.activation(xn2_hi[:, t, :], xn2[:, t, :], ACT.Copy).then_inc(hi_done, 1)

            def h_hi_out(i):
                act.wait_ge(xn2_turned, i * 2 + 1)
                nc.scalar.activation(h_t[:, 0, :, :], mbank[0][:, :].bitcast(F16), ACT.Copy).then_inc(h_hi_done, 1)

            def relu_hi(n, use):
                act.wait_ge(bank_summed, n * USES + use + 1)
                r = r0 if use < NF else r1
                nc.scalar.activation(r[:, 0, use % NF, :], fbank[use % FBANKS][:, :], ACT.Relu)\
                    .then_inc(relu_hi_done, 1)

            act.dma_start(small_rows[0:COORDS * ND, :], w3d.rearrange("c (a p) -> (c a) p", p=P))\
                .then_inc(small_loaded, 16)
            act.dma_start(small_rows[COORDS * ND:, :], bv.rearrange("(a p) -> a p", p=P)).then_inc(small_loaded, 16)
            act.dma_start(b3d_wide[:, :], spread(b3d)).then_inc(rows_loaded, 16)
            for j, s in enumerate((s0, s1, s2)):
                act.dma_start(scales[:, j:j + 1], spread(s)).then_inc(scales_loaded, 16)
            act.dma_start(bo_wide[:, :], spread(bo)).then_inc(rows_loaded, 16)

            for c in range(ND):
                act.wait_ge(wo_turned, c + 1)
                nc.scalar.activation(wo_t[:, c, :], mbank[c][:, 0:D], ACT.Copy).then_inc(wo_t_made, 1)
            xn1_hi(0)
            pos_t_out(0)
            for kt in (3, 2, 1):
                squares(0, kt)
            for c in range(ND):
                act.wait_ge(powers_known, 2)
                nc.scalar.activation(wvo[:, 0, c, 0:D], fbank[1 + c][:, 0:D], ACT.Copy, scale=factors[:, 0, 0:1])\
                    .then_inc(weights_hi_made, 1)
            squares(0, 0)
            v_hi(0, 0)
            v_hi(0, 1)
            distance(0, 0)
            v_hi(0, 2)
            v_hi(0, 3)
            distance(0, 1)
            exponent(0, 0)
            exponent(0, 1)
            xn1_hi(1)
            probs_high(0)
            act.wait_ge(k1_loaded, 16)
            act.wait_ge(factors_made, 3)
            for c in range(W1_ON_POOL, NF):
                nc.scalar.activation(w1[:, c, :], k1_bits[:, c, :], ACT.Identity, bias=w_factors[:, 2:3],
                                     scale=w_factors[:, 1:2]).then_inc(w1_made, 1)
            v_hi(1, 0)
            v_hi(1, 1)
            high_part(0)
            v_hi(1, 2)
            v_hi(1, 3)
            h_hi_out(0)

            def body(n, attention, ahead):
                relu_hi(n, 0)
                relu_hi(n, 1)
                if attention:
                    pos_t_out(n + 1)
                relu_hi(n, 2)
                relu_hi(n, 3)
                relu_hi(n, 4)
                for m, c in ((5, 0), (6, 1), (7, 2)):
                    if attention:
                        squares(n + 1, NT - 1, [c])
                    relu_hi(n, m)
                if attention:
                    squares(n + 1, 2)
                    squares(n + 1, 1)
                    squares(n + 1, 0)
                relu_hi(n, NF)
                if attention:
                    distance(n + 1, 0)
                    distance(n + 1, 1)
                relu_hi(n, NF + 1)
                if attention:
                    exponent(n + 1, 0)
                    exponent(n + 1, 1)
                relu_hi(n, NF + 2)
                if attention:
                    probs_high(n + 1)
                for m in range(3, 7):
                    relu_hi(n, NF + m)
                if ahead:
                    xn1_hi(n + 2)
                if attention:
                    high_part(n + 1)
                relu_hi(n, NF + 7)
                if attention:
                    h_hi_out(n + 1)
                if ahead:
                    for t in range(NT):
                        v_hi(n + 2, t)

            with act.Fori(0, BATCHES - 2) as n:
                body(n, True, True)
            body(BATCHES - 2, True, False)
            body(BATCHES - 1, False, False)

        @block.vector
        def _(dve):
            def moments(i, stats, stats_done, mean, ve, part, part_done, scale, ve_done):
                dve.wait_ge(stats_done, i * NT + NT)
                nc.vector.tensor_tensor(part[:, 0, :], stats[:, :, 1], stats[:, :, 4], ALU.add).then_inc(part_done, 1)
                nc.vector.tensor_tensor(part[:, 1, :], stats[:, :, 1], stats[:, :, 4], ALU.subtract)\
                    .then_inc(part_done, 1)
                nc.vector.scalar_tensor_tensor(out=part[:, 2, :], in0=stats[:, :, 2], scalar=D * EPS,
                                               in1=stats[:, :, 5], op0=ALU.add, op1=ALU.add).then_inc(part_done, 1)
                dve.wait_ge(part_done, i * 5 + 2)
                nc.vector.scalar_tensor_tensor(out=part[:, 3, :], in0=part[:, 1, :], scalar=0.25 * scale,
                                               in1=part[:, 1, :], op0=ALU.mult, op1=ALU.mult).then_inc(part_done, 1)
                nc.vector.tensor_scalar(mean[:, :], part[:, 0, :], 0.5, None, ALU.mult).then_inc(part_done, 1)
                dve.wait_ge(part_done, i * 5 + 4)
                nc.vector.scalar_tensor_tensor(out=ve[:, :], in0=part[:, 2, :], scalar=scale / D,
                                               in1=part[:, 3, :], op0=ALU.mult, op1=ALU.add).then_inc(ve_done, 1)

            def ln1(i):
                dve.wait_ge(x_loaded, i * 16 + 16)
                for t in range(NT):
                    nc.vector.bn_stats(stats1[:, t, :], x_in[:, t, :]).then_inc(stats1_done, 1)
                moments(i, stats1, stats1_done, mean1, ve1, part1, part1_done, XN_SCALE ** -2, ve1_done)

            def normalize1(i):
                dve.wait_ge(rstd1_done, i * 1 + 1)
                dve.wait_ge(part1_done, i * 5 + 5)
                if not (isinstance(i, int) and i == 0):
                    dve.wait_ge(xn1_turned, i * ND)
                for t in range(NT):
                    nc.vector.tensor_scalar(xn1[:, t, :], x_in[:, t, :], mean1[:, t:t + 1], rstd1[:, t:t + 1],
                                            ALU.subtract, ALU.mult).then_inc(xn1_done, 1)

            def xn1_lo(i):
                for c in range(ND):
                    dve.wait_ge(xn1_t_hi_done, i * ND + c + 1)
                    nc.vector.tensor_tensor(xn1_t[:, 1, c, :], mbank[c][:, :], xn1_t[:, 0, c, :], ALU.subtract)\
                        .then_inc(xn1_t_done, 1)

            def v_lo(i, t):
                dve.wait_ge(v_hi_done, i * NT + t + 1)
                nc.vector.scalar_tensor_tensor(out=v[:, 1, t, 0:D], in0=mbank[t % 2][:, 0:D],
                                               scalar=V_SCALE / (XN_SCALE * W_SCALE), in1=v[:, 0, t, 0:D],
                                               op0=ALU.mult, op1=ALU.subtract).then_inc(v_done, 1)

            def positions(i, t, sums, spread_bias, tiles):
                if t == 0 and not (isinstance(i, int) and i == 0):
                    dve.wait_ge(squares_done, i * NS_OPS)
                nc.vector.scalar_tensor_tensor(out=pos[:, t:t + tiles, :], in0=sums, scalar=factors[:, 1, 1:2],
                                               in1=spread_bias, op0=ALU.mult, op1=ALU.add).then_inc(pos_done, tiles)

            def positions_of(i, t):
                dve.wait_ge(v_summed, i * NT + t + 1)
                positions(i, t, mbank[t % 2][:, D:VC], b3d_wide[:, :], 1)

            def split_pos(i):
                dve.wait_ge(pos_done, i * NT + NT)
                nc.vector.tensor_scalar(pos_neg[:, :, :], pos[:, :, :], -1.0, None, ALU.mult).then_inc(pos_neg_done, 1)
                nc.vector.tensor_copy(pos_parts[:, :, 0, :], pos[:, :, :]).then_inc(split_done, 1)
                dve.wait_ge(split_done, i * 5 + 1)
                nc.vector.tensor_tensor(pos_rest[:, 0], pos[:, :, :], pos_parts[:, :, 0, :], ALU.subtract)\
                    .then_inc(split_done, 1)
                dve.wait_ge(split_done, i * 5 + 2)
                nc.vector.tensor_copy(pos_parts[:, :, 1, :], pos_rest[:, 0]).then_inc(split_done, 1)
                dve.wait_ge(split_done, i * 5 + 3)
                nc.vector.tensor_tensor(pos_rest[:, 1], pos_rest[:, 0], pos_parts[:, :, 1, :], ALU.subtract)\
                    .then_inc(split_done, 1)
                dve.wait_ge(split_done, i * 5 + 4)
                nc.vector.tensor_copy(pos_parts[:, :, 2, :], pos_rest[:, 1]).then_inc(split_done, 1)

            def sums(i, h):
                a, b = CHUNKS[h]
                dve.wait_ge(squares_done, i * NS_OPS + NS_OPS - (COORDS if h == 0 else 0))
                nc.vector.scalar_tensor_tensor(out=sum_xy[:, a:b], in0=square[:, 0, a:b], scalar=TINY,
                                               in1=square[:, 1, a:b], op0=ALU.max, op1=ALU.add)\
                    .then_inc(sum_xy_done, 1)
                dve.wait_ge(sum_xy_done, i * 2 + h + 1)
                nc.vector.tensor_tensor(sum_xyz[:, a:b], sum_xy[:, a:b], square[:, 2, a:b], ALU.add)\
                    .then_inc(sum_xyz_done, 1)

            def probs_low(i):
                for j, kt in enumerate(KEY_ORDER):
                    dve.wait_ge(probs_hi_done, i * NT + j + 1)
                    row = slice(ROW[kt], ROW[kt] + SEQ - kt * P)
                    nc.vector.scalar_tensor_tensor(out=probs_lo[:, row], in0=probs[:, row], scalar=E_SCALE,
                                                   in1=probs_hi[:, row], op0=ALU.mult, op1=ALU.subtract)\
                        .then_inc(probs_done, 1)

            def residual(i, t):
                dve.wait_ge(attn_summed, i * NT + t + 1)
                nc.vector.reciprocal(rsum[:, 0, t:t + 1], mbank[t % 2][:, D:D + 1]).then_inc(rsum_done, 1)
                dve.wait_ge(rsum_done, i * 2 * NT + 2 * t + 1)
                nc.vector.tensor_scalar(rsum[:, 1, t:t + 1], rsum[:, 0, t:t + 1], factors[:, 0, 1:2], None, ALU.mult)\
                    .then_inc(rsum_done, 1)
                dve.wait_ge(biased, i * NT + t + 1)
                if t == 0 and not (isinstance(i, int) and i == 0):
                    dve.wait_ge(x1_moved, i * 16)
                dve.wait_ge(rsum_done, i * 2 * NT + 2 * t + 2)
                nc.vector.scalar_tensor_tensor(out=x1_new[:, t, :], in0=mbank[t % 2][:, 0:D],
                                               scalar=rsum[:, 1, t:t + 1], in1=x_biased[:, t, :],
                                               op0=ALU.mult, op1=ALU.add).then_inc(x1_done, 1)

            def ln2_stats(i, t):
                dve.wait_ge(x1_done, i * NT + t + 1)
                nc.vector.bn_stats(stats2[:, t, :], x1_new[:, t, :]).then_inc(stats2_done, 1)

            def ln2_var(i):
                moments(i, stats2, stats2_done, mean2, ve2, part2, part2_done, XN_SCALE ** -2, ve2_done)

            def normalize2(i):
                dve.wait_ge(rstd2_done, i * 1 + 1)
                dve.wait_ge(part2_done, i * 5 + 5)
                if not (isinstance(i, int) and i == 0):
                    dve.wait_ge(lo_done, i * NT)
                for t in range(NT):
                    nc.vector.tensor_scalar(xn2[:, t, :], x1_new[:, t, :], mean2[:, t:t + 1], rstd2[:, t:t + 1],
                                            ALU.subtract, ALU.mult).then_inc(xn2_done, 1)

            def low_part(i):
                for t in range(NT):
                    dve.wait_ge(hi_done, i * NT + t + 1)
                    nc.vector.tensor_tensor(xn2_lo[:, t, :], xn2[:, t, :], xn2_hi[:, t, :], ALU.subtract)\
                        .then_inc(lo_done, 1)

            def h_lo_out(i):
                dve.wait_ge(xn2_turned, i * 2 + 2)
                nc.vector.tensor_copy(h_t[:, 1, :, :], mbank[1][:, :].bitcast(F16)).then_inc(h_lo_done, 1)

            def relu_lo(n, use):
                r = r0 if use < NF else r1
                dve.wait_ge(relu_hi_done, n * 2 * NF + use + 1)
                nc.vector.scalar_tensor_tensor(out=r[:, 1, use % NF, :], in0=fbank[use % FBANKS][:, :], scalar=0.0,
                                               in1=r[:, 0, use % NF, :], op0=ALU.max, op1=ALU.subtract)\
                    .then_inc(bank_free, 1)

            def finish(n, half):
                use = 2 * NF + half
                dve.wait_ge(bank_summed, n * USES + use + 1)
                if half == 0:
                    dve.wait_ge(x1_moved, n * 16 + 16)
                t = 2 * half
                z = fbank[use % FBANKS][:, :].rearrange("p (t d) -> p t d", d=D)
                nc.vector.scalar_tensor_tensor(out=y[:, t:t + 2, :], in0=z, scalar=out_factor[:, 1:2],
                                               in1=x1_cur[:, t:t + 2, :], op0=ALU.mult, op1=ALU.add)\
                    .then_inc(bank_free, 1)

            def powers_of(j):
                dve.wait_ge(largest_turned, 2 - j)
                row = largest_row[:, j:j + 1]
                up, down = powers[:, j, 0:1], powers[:, j, 1:2]
                at = (1 - j) * 5
                nc.vector.reduce_max(row, fbank[0][0:1, 0:P], AX_X).then_inc(power_steps, 1)
                dve.wait_ge(power_steps, at + 1)
                nc.vector.tensor_scalar(row, row, TINY, None, ALU.max).then_inc(power_steps, 1)
                dve.wait_ge(power_steps, at + 2)
                nc.vector.tensor_scalar(down.bitcast(I32), row.bitcast(I32), 0xFF << 23, None, ALU.bitwise_and)\
                    .then_inc(power_steps, 1)
                dve.wait_ge(power_steps, at + 3)
                nc.vector.tensor_scalar(up.bitcast(I32), down.bitcast(I32), -1.0, float(254 << 23),
                                        ALU.mult, ALU.add).then_inc(power_steps, 1)
                dve.wait_ge(power_steps, at + 4)
                nc.vector.tensor_scalar(up, up, W_SCALE, None, ALU.mult)
                nc.vector.tensor_scalar(down, down, 1.0 / V_SCALE if j == 0 else 1.0 / (XN_SCALE * W_SCALE), None,
                                        ALU.mult).then_inc(power_steps, 1)
                dve.wait_ge(powers_spread, 2 - j)
                nc.vector.tensor_copy(factors[:, j, :], fbank[0][:, P:P + 2]).then_inc(powers_known, 1)

            nc.vector.memset(ones_row[:, :], 1.0).then_inc(ones_made, 1)
            nc.vector.memset(v[:, 1, :, D:D + 1], 0.0).then_inc(ones_made, 1)
            nc.vector.memset(v[:, 0, :, D:D + 1], 1.0).then_inc(bank_free, FBANKS)
            ln1(0)
            dve.wait_ge(small_turned, 1)
            nc.vector.tensor_copy(small_cols[:, :], fbank[0][:, 0:ND * (COORDS + 1)]).then_inc(small_made, 1)
            dve.wait_ge(small_made, 1)
            nc.vector.tensor_reduce(largest[:, 1:2], small_cols[:, 0:ND * COORDS], AX_X, ALU.max,
                                    apply_absolute_value=True).then_inc(largest_found, 1)
            for c in range(ND):
                j = ND * COORDS + c
                nc.vector.tensor_copy(bv_wide[:, c, :], small_cols[:, j:j + 1].to_broadcast([P, P]))\
                    .then_inc(bv_spread, 1)
            normalize1(0)
            powers_of(1)
            dve.wait_ge(powers_known, 1)
            w3d_in = small_cols[:, 0:ND * COORDS].rearrange("p (c a) -> p a c", a=ND)
            nc.vector.tensor_scalar(wvo[:, 0, :, D:VC], w3d_in, factors[:, 1, 0:1], None, ALU.mult)\
                .then_inc(w3d_made, 1)
            dve.wait_ge(w3d_made, 1)
            nc.vector.scalar_tensor_tensor(out=wvo[:, 1, :, D:VC], in0=w3d_in, scalar=factors[:, 1, 0:1],
                                           in1=wvo[:, 0, :, D:VC], op0=ALU.mult, op1=ALU.subtract)\
                .then_inc(w3d_made, 1)
            xn1_lo(0)
            dve.wait_ge(rows_loaded, 32)
            dve.wait_ge(pos_summed, 1)
            positions(0, 0, fbank[0][:, 2 * P:2 * P + NT * COORDS].rearrange("p (t c) -> p t c", c=COORDS),
                      b3d_wide[:, :].rearrange("p (a c) -> p a c", a=1).to_broadcast([P, NT, COORDS]), NT)
            split_pos(0)
            for c in range(ND):
                dve.wait_ge(wvo_summed, c + 1)
                nc.vector.tensor_reduce(largest_of_tile[:, c:c + 1], fbank[1 + c][:, 0:D], AX_X, ALU.max,
                                        apply_absolute_value=True).then_inc(abs_done, 1)
            dve.wait_ge(abs_done, ND)
            nc.vector.reduce_max(largest[:, 0:1], largest_of_tile[:, :], AX_X).then_inc(largest_found, 1)
            dve.wait_ge(scales_loaded, 48)
            nc.vector.tensor_scalar(signs[:, :], scales[:, 0:2], 0.0, 2.0, ALU.is_ge, ALU.mult).then_inc(signs_made, 1)
            dve.wait_ge(signs_made, 1)
            nc.vector.tensor_scalar(signs[:, :], signs[:, :], -1.0, None, ALU.add).then_inc(signs_made, 1)
            dve.wait_ge(signs_made, 2)
            nc.vector.tensor_tensor(magnitudes[:, :], scales[:, 0:2], signs[:, :], ALU.mult).then_inc(signs_made, 1)
            nc.vector.tensor_scalar(w_factors[:, 0:1], signs[:, 0:1], 2.0 * W0_SCALE, None, ALU.mult)\
                .then_inc(factors_made, 1)
            nc.vector.tensor_scalar(w_factors[:, 1:2], signs[:, 1:2], 2.0 * W1_SCALE, None, ALU.mult)\
                .then_inc(factors_made, 1)
            nc.vector.tensor_scalar(w_factors[:, 2:3], signs[:, 1:2], -W1_SCALE, None, ALU.mult)\
                .then_inc(factors_made, 1)
            powers_of(0)
            for c in range(ND):
                dve.wait_ge(weights_hi_made, c + 1)
                nc.vector.scalar_tensor_tensor(out=wvo[:, 1, c, 0:D], in0=fbank[1 + c][:, 0:D],
                                               scalar=factors[:, 0, 0:1], in1=wvo[:, 0, c, 0:D],
                                               op0=ALU.mult, op1=ALU.subtract).then_inc(wvo_made, 1)
            dve.wait_ge(wvo_summed, ND + 1)
            nc.vector.tensor_tensor(v_bias[:, :], fbank[0][:, D:2 * D], bo_wide[:, :], ALU.add)\
                .then_inc(v_bias_made, 1)
            ln1(1)
            dve.wait_ge(signs_made, 3)
            nc.vector.scalar_tensor_tensor(out=out_factor[:, 0:1], in0=magnitudes[:, 0:1], scalar=OUT_SCALE,
                                           in1=magnitudes[:, 1:2], op0=ALU.mult, op1=ALU.mult)\
                .then_inc(out_factor_made, 1)
            dve.wait_ge(out_factor_made, 1)
            nc.vector.tensor_tensor(out_factor[:, 1:2], out_factor[:, 0:1], scales[:, 2:3], ALU.mult)\
                .then_inc(out_factor_made, 1)
            dve.wait_ge(out_factor_made, 2)
            sums(0, 0)
            v_lo(0, 0)
            v_lo(0, 1)
            sums(0, 1)
            normalize1(1)
            v_lo(0, 2)
            v_lo(0, 3)
            xn1_lo(1)
            probs_low(0)
            dve.wait_ge(k0_loaded, 16)
            dve.wait_ge(factors_made, 3)
            nc.vector.tensor_tensor(w0_diff[:, :, :], k0_bits[:, 0:ND, :], k0_bits[:, ND:2 * ND, :], ALU.subtract)\
                .then_inc(w0_diffed, 1)
            for t in range(NT):
                residual(0, t)
                ln2_stats(0, t)
            ln2_var(0)
            v_lo(1, 0)
            positions_of(1, 0)
            v_lo(1, 1)
            positions_of(1, 1)
            normalize2(0)
            low_part(0)
            v_lo(1, 2)
            positions_of(1, 2)
            v_lo(1, 3)
            positions_of(1, 3)
            dve.wait_ge(w0_diffed, 1)
            nc.vector.tensor_scalar(w0[:, :, :], w0_diff[:, :, :], w_factors[:, 0:1], None, ALU.mult)\
                .then_inc(w0_made, 1)
            h_lo_out(0)
            split_pos(1)

            def body(n, attention, ahead):
                for m in range(NF):
                    relu_lo(n, m)
                if attention:
                    sums(n + 1, 0)
                relu_lo(n, NF)
                if attention:
                    sums(n + 1, 1)
                if ahead:
                    ln1(n + 2)
                relu_lo(n, NF + 1)
                if ahead:
                    normalize1(n + 2)
                relu_lo(n, NF + 2)
                if attention:
                    probs_low(n + 1)
                relu_lo(n, NF + 3)
                relu_lo(n, NF + 4)
                if attention:
                    for t in range(2):
                        residual(n + 1, t)
                        ln2_stats(n + 1, t)
                relu_lo(n, NF + 5)
                if attention:
                    for t in range(2, NT):
                        residual(n + 1, t)
                        ln2_stats(n + 1, t)
                    ln2_var(n + 1)
                relu_lo(n, NF + 6)
                if attention:
                    normalize2(n + 1)
                if ahead:
                    xn1_lo(n + 2)
                if attention:
                    low_part(n + 1)
                relu_lo(n, NF + 7)
                if attention:
                    h_lo_out(n + 1)
                finish(n, 0)
                if ahead:
                    for t in range(NT):
                        v_lo(n + 2, t)
                        positions_of(n + 2, t)
                    split_pos(n + 2)
                finish(n, 1)

            with dve.Fori(0, BATCHES - 2) as n:
                body(n, True, True)
            body(BATCHES - 2, True, False)
            body(BATCHES - 1, False, False)

        @block.tensor
        def _(pe):
            def turn_xn1(i):
                pe.wait_ge(xn1_done, i * NT + NT)
                for c in range(ND):
                    for t in range(NT):
                        last = nc.tensor.transpose(mbank[c][:, t * P:(t + 1) * P], xn1[:, t, c * P:(c + 1) * P],
                                                   ident[:, :])
                    last.then_inc(xn1_turned, 1)

            PASSES = ((0, 0), (0, 1), (1, 0))

            def values(i, t, columns=VC):
                if t == 0:
                    pe.wait_ge(xn1_t_done, i * ND + ND)
                if t >= 2:
                    pe.wait_ge(v_done, i * NT + t - 1)
                    if columns > D:
                        pe.wait_ge(pos_done, i * NT + t - 1)
                for c in range(ND):
                    for a, b in PASSES:
                        last = nc.tensor.matmul(mbank[t % 2][:, 0:columns], xn1_t[:, a, c, t * P:(t + 1) * P],
                                                wvo[:, b, c, 0:columns], start=(c == 0 and (a, b) == (0, 0)),
                                                stop=(c == ND - 1 and (a, b) == PASSES[-1]))
                last.then_inc(v_summed, 1)

            def turn_pos(i):
                pe.wait_ge(split_done, i * 5 + 5)
                pt = mbank[0][0:PARTS * COORDS, 0:SEQ // 2].bitcast(BF16)
                for t in range(NT):
                    last = nc.tensor.transpose(pt[:, t * P:(t + 1) * P],
                                               pos_parts[:, t].rearrange("p a c -> p (a c)"), identb[:, :])
                last.then_inc(pos_turned, 1)

            def spread_coords(i):
                pe.wait_ge(pos_t_done, i * 1 + 1)
                if not (isinstance(i, int) and i == 0):
                    pe.wait_ge(squares_done, i * NS_OPS)
                for c in range(COORDS):
                    last = nc.tensor.matmul(coord_bank[c][:, :], pick[:, c, :], pos_t[:, :], start=True, stop=True)
                last.then_inc(coords_spread, 1)

            def attend(i, qt):
                if qt == 0:
                    pe.wait_ge(probs_done, i * NT + NT)
                    pe.wait_ge(v_done, i * NT + NT)
                if qt >= 2:
                    pe.wait_ge(x1_done, i * NT + qt - 1)
                for kt in range(qt + 1):
                    col = ROW[kt] + (qt - kt) * P
                    for a, b in PASSES:
                        e = (probs_hi, probs_lo)[a]
                        last = nc.tensor.matmul(mbank[qt % 2][:, 0:D + 1], e[:, col:col + P], v[:, b, kt, :],
                                                start=(kt == 0 and (a, b) == (0, 0)),
                                                stop=(kt == qt and (a, b) == PASSES[-1]))
                last.then_inc(attn_summed, 1)

            def turn_xn2(i):
                for part, source, done in ((0, xn2_hi, hi_done), (1, xn2_lo, lo_done)):
                    pe.wait_ge(done, i * NT + NT)
                    turned = mbank[part][:, :].bitcast(F16)
                    for c in range(ND):
                        for t in range(NT):
                            at = c * SEQ + t * P
                            last = nc.tensor.transpose(turned[:, at:at + P], source[:, t, c * P:(c + 1) * P],
                                                       ident16[:, :])
                    last.then_inc(xn2_turned, 1)

            def hidden(n, use, weights, source, k_tiles):
                m = use % NF
                if m or weights is w0:
                    pe.wait_ge(bank_free, n * USES + use + 1)
                for k in range(k_tiles):
                    if weights is w1 and m == 0:
                        pe.wait_ge(bank_free, n * USES + max(k, use - FBANKS) + 1 + FBANKS)
                    for part in range(2):
                        last = nc.tensor.matmul(fbank[use % FBANKS][:, :], weights[:, k, m * P:(m + 1) * P],
                                                source[:, part, k, :], start=(k == 0 and part == 0),
                                                stop=(k == k_tiles - 1 and part == 1))
                last.then_inc(bank_summed, 1)

            def layer0(n, m):
                if m == 0:
                    pe.wait_ge(h_hi_done, n * 1 + 1)
                    pe.wait_ge(h_lo_done, n * 1 + 1)
                hidden(n, m, w0, h_t, ND)

            def layer1(n, m):
                hidden(n, NF + m, w1, r0, NF)

            def layer2(n, half, tiles=(0, 1)):
                use = 2 * NF + half
                if half == 1 and 0 in tiles:
                    pe.wait_ge(bank_free, n * USES + use + 1)
                for s in tiles:
                    t = 2 * half + s
                    for k in range(NF):
                        if half == 0 and s == 0:
                            pe.wait_ge(bank_free, n * USES + NF + max(k, NF - FBANKS) + 1 + FBANKS)
                        for part in range(2):
                            last = nc.tensor.matmul(fbank[use % FBANKS][:, s * D:(s + 1) * D],
                                                    r1[:, part, k, t * P:(t + 1) * P], w2[:, k, :],
                                                    start=(k == 0 and part == 0), stop=(k == NF - 1 and part == 1))
                if 1 in tiles:
                    last.then_inc(bank_summed, 1)

            def spread_powers(j):
                pe.wait_ge(largest_found, 2 - j)
                nc.tensor.transpose(fbank[0][0:1, 0:P], largest[:, j:j + 1], ident[:, :]).then_inc(largest_turned, 1)
                pe.wait_ge(power_steps, (2 - j) * 5)
                nc.tensor.matmul(fbank[0][:, P:P + 2], ones_row[:, :], powers[:, j, :], start=True, stop=True)\
                    .then_inc(powers_spread, 1)

            def wvo_tile(c):
                for j in range(ND):
                    last = nc.tensor.matmul(fbank[1 + c][:, 0:D], wv_rows[:, j, c * P:(c + 1) * P], wo_t[:, j, :],
                                            start=(j == 0), stop=(j == ND - 1))
                last.then_inc(wvo_summed, 1)

            pe.wait_ge(ident_made, 1)
            pe.wait_ge(small_loaded, 32)
            nc.tensor.transpose(fbank[0][:, 0:ND * (COORDS + 1)], small_rows[:, :],
                                ident[0:ND * (COORDS + 1), 0:ND * (COORDS + 1)]).then_inc(small_turned, 1)
            pe.wait_ge(wo_loaded, 16)
            for c in range(ND):
                for o in range(ND):
                    last = nc.tensor.transpose(mbank[c][:, o * P:(o + 1) * P], wo_rows[:, o, c * P:(c + 1) * P],
                                               ident[:, :])
                last.then_inc(wo_turned, 1)
            pe.wait_ge(ones_made, 2)
            spread_powers(1)
            pe.wait_ge(wo_t_made, ND)
            turn_xn1(0)
            pe.wait_ge(w3d_made, 2)
            pe.wait_ge(xn1_t_done, ND)
            for t in range(NT):
                at = 2 * P + t * COORDS
                for c in range(ND):
                    for a, b in PASSES:
                        last = nc.tensor.matmul(fbank[0][:, at:at + COORDS], xn1_t[:, a, c, t * P:(t + 1) * P],
                                                wvo[:, b, c, D:VC], start=(c == 0 and (a, b) == (0, 0)),
                                                stop=(c == ND - 1 and (a, b) == PASSES[-1]))
            last.then_inc(pos_summed, 1)
            pe.wait_ge(wv_loaded, 16)
            wvo_tile(0)
            pe.wait_ge(ident_made, 3)
            turn_pos(0)
            wvo_tile(1)
            pe.wait_ge(consts_made, 1 + PARTS)
            spread_coords(0)
            spread_powers(0)
            pe.wait_ge(bv_spread, ND)
            pe.wait_ge(powers_known, 2)
            for j in range(ND):
                last = nc.tensor.matmul(fbank[0][:, D:2 * D], bv_wide[:, j, :], wo_t[:, j, :],
                                        start=(j == 0), stop=(j == ND - 1))
            last.then_inc(wvo_summed, 1)
            pe.wait_ge(wvo_made, ND)
            pe.wait_ge(pos_t_done, 1)
            for t in range(NT):
                values(0, t, D)
            pe.wait_ge(v_done, NT)
            turn_xn1(1)
            pe.wait_ge(xn1_t_done, 2 * ND)
            for qt in range(NT):
                attend(0, qt)
            pe.wait_ge(x1_done, NT - 1)
            values(1, 0)
            pe.wait_ge(x1_done, NT)
            values(1, 1)
            values(1, 2)
            values(1, 3)
            pe.wait_ge(v_done, 2 * NT)
            pe.wait_ge(pos_done, 2 * NT)
            turn_xn2(0)
            pe.wait_ge(w0_made, 1)
            pe.wait_ge(w1_made, NF)
            pe.wait_ge(w2_made, 1)

            def body(n, attention, ahead):
                layer0(n, 0)
                layer0(n, 1)
                if attention:
                    turn_pos(n + 1)
                layer0(n, 2)
                layer0(n, 3)
                if attention:
                    spread_coords(n + 1)
                for m in range(4, NF):
                    layer0(n, m)
                for m in range(0, 5):
                    layer1(n, m)
                if attention:
                    attend(n + 1, 0)
                    attend(n + 1, 1)
                layer1(n, 5)
                if attention:
                    attend(n + 1, 2)
                    attend(n + 1, 3)
                layer1(n, 6)
                if ahead:
                    pe.wait_ge(x1_done, n * NT + 2 * NT)
                    turn_xn1(n + 2)
                layer1(n, 7)
                if attention:
                    if ahead:
                        pe.wait_ge(xn1_t_done, n * ND + 3 * ND)
                    turn_xn2(n + 1)
                layer2(n, 0)
                if ahead:
                    pe.wait_ge(h_hi_done, n * 1 + 2)
                    pe.wait_ge(h_lo_done, n * 1 + 2)
                    values(n + 2, 0)
                    values(n + 2, 1)
                layer2(n, 1, [0])
                if ahead:
                    values(n + 2, 2)
                    values(n + 2, 3)
                layer2(n, 1, [1])

            with pe.Fori(0, BATCHES - 2) as n:
                body(n, True, True)
            body(BATCHES - 2, True, False)
            body(BATCHES - 1, False, False)


INPUTS = ["L0_attn_x", "L0_attn_wv", "L0_attn_bv", "L0_attn_wo", "L0_attn_bo", "L0_attn_w3d", "L0_attn_b3d",
          "L0_ffn_k0", "L0_ffn_k1", "L0_ffn_k2", "L0_ffn_s0", "L0_ffn_s1", "L0_ffn_s2"]


def kernel(**inputs):
    import numpy as np
    import concourse.bacc as bacc
    from concourse.bass_utils import run_bass_kernel_spmd

    nc = bacc.Bacc("TRN2", target_bir_lowering=False, num_devices=1)
    arrays, args = {}, []
    for name in INPUTS:
        a = np.ascontiguousarray(inputs[name])
        if a.ndim == 0:
            a = a.reshape(1)
        arrays[name + "_dram"] = a
        args.append(nc.dram_tensor(name + "_dram", a.shape, mybir.dt.from_np(a.dtype), kind="ExternalInput").ap())
    shape = inputs["L0_attn_x"].shape
    args.append(nc.dram_tensor("out_dram", shape, F32, kind="ExternalOutput").ap())
    block_kernel(nc, *args)
    result = run_bass_kernel_spmd(nc, [arrays], core_ids=[0])
    return result.results[0]["out_dram"]
```

```python
from contextlib import ExitStack

import concourse.bass as bass
from concourse import mybir

ALU = mybir.AluOpType
ACT = mybir.ActivationFunctionType
F32 = mybir.dt.float32
F16 = mybir.dt.float16
BF16 = mybir.dt.bfloat16
U8 = mybir.dt.uint8
I32 = mybir.dt.int32
AX_X = mybir.AxisListType.X

P = 128
HEADS = 16
EPS = 1e-5
TINY = 2.0 ** -100
XN_SCALE = 2.0 ** 10
W0_SCALE = 2.0 ** -4
W1_SCALE = 2.0 ** -10
OUT_SCALE = 2.0 ** 4 * 4.0
W_SCALE = 2.0 ** 14
V_SCALE = 2.0 ** 6
E_SCALE = 2.0 ** 15
FBANKS = 3


def block_kernel(nc, x, x_turned, wv, bv, wo, bo, w3d, b3d, k0, k1, k2, s0, s1, s2, coords, norms, out):
    BATCHES, SEQ, D = x.shape
    FF = k1.shape[0]
    NT = SEQ // P
    ND = D // P
    NF = FF // P
    COORDS = w3d.shape[0]
    PARTS = 3
    SCORE_SCALE = 1.0 / (D // HEADS) ** 0.5
    USES = 2 * NF + NT // 2
    VC = D + COORDS
    ROW = [sum(SEQ - j * P for j in range(kt)) for kt in range(NT)]
    NS = ROW[-1] + SEQ - (NT - 1) * P
    NS_OPS = NT * COORDS
    EARLY = (3, 2)
    W1_ON_POOL = NF - 2
    KEY_ORDER = [*range(1, NT), 0]
    CHUNKS = [(SEQ, NS), (0, SEQ)]
    assert USES % FBANKS == 0 and FF == k0.shape[1] and k0.shape[0] == 2 * D

    with ExitStack() as ctx:
        def sb(name, shape, dt):
            return ctx.enter_context(nc.sbuf_tensor(name, shape, dt))

        def psum(name, shape, dt=F32):
            return ctx.enter_context(nc.psum_tensor(name, shape, dt))

        def sem(name):
            return ctx.enter_context(nc.semaphore(name))

        ident = sb("ident", [P, P], F32)
        identb = sb("identb", [P, P], BF16)
        causal = sb("causal", [P, P], F32)
        pick = sb("pick", [PARTS * COORDS, COORDS, P], BF16)
        neg_half = sb("neg_half", [P, NT], F32)
        wo_rows = sb("wo_rows", [P, ND, D], F32)
        wv_rows = sb("wv_rows", [P, ND, D], F32)
        small_rows = sb("small_rows", [ND * (COORDS + 1), P], F32)
        small_cols = sb("small_cols", [P, ND * (COORDS + 1)], F32)
        largest_of_tile = sb("largest_of_tile", [P, ND], F32)
        ones_row = sb("ones_row", [1, P], F32)
        first_sqrt = sb("first_sqrt", [1, 1], F32)
        largest = sb("largest", [P, 2], F32)
        largest_row = sb("largest_row", [1, 2], F32)
        powers = sb("powers", [1, 2, 2], F32)
        factors = sb("factors", [P, 2, 2], F32)
        bv_wide = sb("bv_wide", [P, ND, P], F32)
        wo_t = sb("wo_t", [P, ND, D], F32)
        wvo = sb("wvo", [P, 2, ND, VC], F16)
        bo_wide = sb("bo_wide", [P, D], F32)
        v_bias = sb("v_bias", [P, D], F32)
        b3d_wide = sb("b3d_wide", [P, COORDS], F32)
        scales = sb("scales", [P, 3], F32)
        signs = sb("signs", [P, 2], F32)
        magnitudes = sb("magnitudes", [P, 2], F32)
        w_factors = sb("w_factors", [P, 3], F32)
        out_factor = sb("out_factor", [P, 2], F32)
        k0_bits = sb("k0_bits", [P, 2 * ND, FF], U8)
        k1_bits = sb("k1_bits", [P, NF, FF], U8)
        k2_bits = sb("k2_bits", [P, NF, D], U8)
        w0_minus = sb("w0_minus", [P, ND, FF], F16)
        w0 = sb("w0", [P, ND, FF], F16)
        w1 = sb("w1", [P, NF, FF], F16)
        w2 = sb("w2", [P, NF, D], F16)

        x_in = sb("x_in", [P, NT, D], F32)
        x_keep = sb("x_keep", [P, NT, D], F32)
        stats1 = sb("stats1", [P, NT, 6], F32)
        norm1 = sb("norm1", [P, NT, 2], F32)
        norm_wide = sb("norm_wide", [P, SEQ, 2], F32)
        x_t = sb("x_t", [P, ND, SEQ], F32)
        part1 = sb("part1", [P, 4, NT], F32)
        ve1 = sb("ve1", [P, NT], F32)
        xn1 = sb("xn1", [P, NT, D], F32)
        xn_t = xn1[:, :, :].rearrange("p t d -> p (t d)").rearrange("p (c s) -> p c s", s=SEQ)
        xn1_t = sb("xn1_t", [P, 2, ND, SEQ], F16)
        v = sb("v", [P, 2, NT, D + 1], F16)
        pos = sb("pos", [P, NT, COORDS], F32)
        pos_neg = sb("pos_neg", [P, NT, COORDS], F32)
        pos_rest = sb("pos_rest", [P, 2, NT, COORDS], F32)
        pos_parts = sb("pos_parts", [P, NT, PARTS, COORDS], BF16)
        pos_t = sb("pos_t", [PARTS * COORDS, SEQ], BF16)
        square = sb("square", [P, COORDS, NS], F32)
        early_diff = sb("early_diff", [P, NS - ROW[EARLY[1]]], F32)
        coords_wide = sb("coords_wide", [P, SEQ, COORDS], F32)
        sum_xy = sb("sum_xy", [P, NS], F32)
        sum_xyz = sb("sum_xyz", [P, NS], F32)
        dist = sb("dist", [P, NS], F32)
        probs = sb("probs", [P, NS], F32)
        probs_hi = sb("probs_hi", [P, NS], F16)
        probs_lo = sb("probs_lo", [P, NS], F16)
        rsum = sb("rsum", [P, 2, NT], F32)
        x_biased = sb("x_biased", [P, NT, D], F32)
        x1_new = sb("x1_new", [P, NT, D], F32)
        x1_cur = sb("x1_cur", [P, NT, D], F32)
        stats2 = sb("stats2", [P, NT, 6], F32)
        mean2 = sb("mean2", [P, NT], F32)
        part2 = sb("part2", [P, 4, NT], F32)
        ve2 = sb("ve2", [P, NT], F32)
        rstd2 = sb("rstd2", [P, NT], F32)
        xn2 = sb("xn2", [P, NT, D], F32)

        h_t = sb("h_t", [P, 2, ND, SEQ], F16)
        r0 = sb("r0", [P, 2, NF, SEQ], F16)
        r1 = sb("r1", [P, 2, NF, SEQ], F16)
        y = sb("y", [P, NT, D], F32)

        fbank = [psum(f"fbank{i}", [P, 512]) for i in range(FBANKS)]
        coord_bank = [psum(f"coord_bank{c}", [P, SEQ]) for c in range(COORDS)]
        mbank = [psum(f"mbank{i}", [P, 512]) for i in range(2)]
        early_turn_banks = fbank[1:3]
        early_v_banks = [*coord_bank, coord_bank[0]]

        small_loaded = sem("small_loaded")
        wo_loaded = sem("wo_loaded")
        wv_loaded = sem("wv_loaded")
        rows_loaded = sem("rows_loaded")
        scales_loaded = sem("scales_loaded")
        k0_loaded = sem("k0_loaded")
        k1_loaded = sem("k1_loaded")
        k2_loaded = sem("k2_loaded")
        filled = sem("filled")
        ident_made = sem("ident_made")
        consts_made = sem("consts_made")
        wo_turned = sem("wo_turned")
        wo_t_made = sem("wo_t_made")
        small_turned = sem("small_turned")
        small_made = sem("small_made")
        bv_spread = sem("bv_spread")
        wvo_summed = sem("wvo_summed")
        ones_made = sem("ones_made")
        abs_done = sem("abs_done")
        largest_found = sem("largest_found")
        largest_turned = sem("largest_turned")
        power_steps = sem("power_steps")
        powers_spread = sem("powers_spread")
        powers_known = sem("powers_known")
        weights_hi_made = sem("weights_hi_made")
        w3d_made = sem("w3d_made")
        wvo_made = sem("wvo_made")
        v_bias_made = sem("v_bias_made")
        signs_made = sem("signs_made")
        factors_made = sem("factors_made")
        out_factor_made = sem("out_factor_made")
        w0_scaled = sem("w0_scaled")
        w0_made = sem("w0_made")
        w1_made = sem("w1_made")
        w2_made = sem("w2_made")
        half_loaded = sem("half_loaded")
        x_loaded = sem("x_loaded")
        keep_loaded = sem("keep_loaded")
        stats1_done = sem("stats1_done")
        part1_done = sem("part1_done")
        ve1_done = sem("ve1_done")
        rstd1_done = sem("rstd1_done")
        xn1_done = sem("xn1_done")
        xt_loaded = sem("xt_loaded")
        norm_stored = sem("norm_stored")
        norm_loaded = sem("norm_loaded")
        centered = sem("centered")
        xn_t_done = sem("xn_t_done")
        xn1_turned = sem("xn1_turned")
        xn1_t_hi_done = sem("xn1_t_hi_done")
        xn1_t_done = sem("xn1_t_done")
        v_summed = sem("v_summed")
        pos_summed = sem("pos_summed")
        v_hi_done = sem("v_hi_done")
        v_done = sem("v_done")
        pos_done = sem("pos_done")
        pos_neg_done = sem("pos_neg_done")
        split_done = sem("split_done")
        pos_turned = sem("pos_turned")
        pos_t_done = sem("pos_t_done")
        coords_spread = sem("coords_spread")
        coords_stored = sem("coords_stored")
        coords_loaded = sem("coords_loaded")
        squares_done = sem("squares_done")
        early_diff_done = sem("early_diff_done")
        early_squares_done = sem("early_squares_done")
        sum_xy_done = sem("sum_xy_done")
        sum_xyz_done = sem("sum_xyz_done")
        dist_done = sem("dist_done")
        exp_done = sem("exp_done")
        masked = sem("masked")
        probs_hi_done = sem("probs_hi_done")
        probs_done = sem("probs_done")
        biased = sem("biased")
        attn_summed = sem("attn_summed")
        rsum_done = sem("rsum_done")
        x1_done = sem("x1_done")
        x1_moved = sem("x1_moved")
        stats2_done = sem("stats2_done")
        part2_done = sem("part2_done")
        ve2_done = sem("ve2_done")
        rstd2_done = sem("rstd2_done")
        xn2_done = sem("xn2_done")
        xn2_turned = sem("xn2_turned")
        h_hi_done = sem("h_hi_done")
        h_done = sem("h_done")
        bank_summed = sem("bank_summed")
        relu_hi_done = sem("relu_hi_done")
        bank_free = sem("bank_free")
        y_stored = sem("y_stored")

        block = ctx.enter_context(nc.Block())

        def squares_before(i):
            return i * NS_OPS - len(EARLY)

        def tokens(dram, i):
            return dram[i].rearrange("(t p) d -> p t d", p=P)

        def spread(vector):
            return vector.rearrange("(a n) -> a n", a=1).to_broadcast([P, vector.shape[0]])

        @block.sync
        def _(sp):
            def load_x(i):
                if isinstance(i, int) and i <= 2:
                    sp.wait_ge(xn1_done, i * NT)
                else:
                    sp.wait_ge(stats1_done, i * NT)
                sp.dma_start(x_in[:, :, :], tokens(x, i)).then_inc(x_loaded, 16)

            def load_keep(i):
                if not (isinstance(i, int) and i == 0):
                    sp.wait_ge(biased, i * NT)
                sp.dma_start(x_keep[:, :, :], tokens(x, i)).then_inc(keep_loaded, 16)

            def store_coords(i):
                sp.wait_ge(pos_done, i * NT + NT)
                sp.dma_start(coords[i].rearrange("(t p) c -> p t c", p=P), pos[:, :, :]).then_inc(coords_stored, 16)

            def load_coords(i):
                sp.wait_ge(coords_stored, i * 16)
                sp.wait_ge(squares_done, squares_before(i))
                flat = coords[i].rearrange("s c -> (s c)").rearrange("(a n) -> a n", a=1)
                sp.dma_start(coords_wide[:, :, :].rearrange("p s c -> p (s c)"),
                             flat.to_broadcast([P, COORDS * SEQ])).then_inc(coords_loaded, 16)

            def load_x_t(i):
                if not (isinstance(i, int) and i == 2):
                    sp.wait_ge(xn_t_done, (i - 2) * ND)
                sp.dma_start(x_t[:, :, :], x_turned[i].rearrange("(c p) s -> p c s", p=P)).then_inc(xt_loaded, 16)

            def spread_norm(i):
                if not (isinstance(i, int) and i == 2):
                    sp.wait_ge(xn_t_done, (i - 2) * ND)
                sp.wait_ge(part1_done, i * 5 + 5)
                sp.wait_ge(rstd1_done, i * 1 + 1)
                sp.dma_start(norms[i].rearrange("(t p) k -> p t k", p=P), norm1[:, :, :]).then_inc(norm_stored, 16)
                sp.wait_ge(norm_stored, i * 16 - 16)
                flat = norms[i].rearrange("s k -> (s k)").rearrange("(a n) -> a n", a=1)
                sp.dma_start(norm_wide[:, :, :].rearrange("p s k -> p (s k)"),
                             flat.to_broadcast([P, 2 * SEQ])).then_inc(norm_loaded, 16)

            def move_x1(i):
                sp.dma_start(x1_cur[:, :, :], x1_new[:, :, :]).then_inc(x1_moved, 16)

            def store_y(n, half):
                sp.wait_ge(bank_free, n * USES + 2 * NF + half + 1 + FBANKS)
                t = 2 * half
                sp.dma_start(tokens(out, n)[:, t:t + 2, :], y[:, t:t + 2, :]).then_inc(y_stored, 16)

            sp.dma_start(x_in[:, 0:NT // 2, :], tokens(x, 0)[:, 0:NT // 2, :]).then_inc(half_loaded, 16)
            sp.dma_start(x_in[:, NT // 2:, :], tokens(x, 0)[:, NT // 2:, :]).then_inc(x_loaded, 16)
            sp.dma_start(wo_rows[:, :, :], wo.rearrange("(c p) d -> p c d", p=P)).then_inc(wo_loaded, 16)
            sp.dma_start(wv_rows[:, :, :], wv.rearrange("(c p) d -> p c d", p=P)).then_inc(wv_loaded, 16)
            for j, s in enumerate((s0, s1, s2)):
                sp.dma_start(scales[:, j:j + 1], spread(s)).then_inc(scales_loaded, 16)
            sp.dma_start(bo_wide[:, :], spread(bo)).then_inc(rows_loaded, 16)
            sp.dma_start(k1_bits[:, :, :], k1.rearrange("(c p) f -> p c f", p=P)).then_inc(k1_loaded, 16)
            sp.dma_start(k0_bits[:, :, :], k0.rearrange("(c p) f -> p c f", p=P)).then_inc(k0_loaded, 16)
            sp.dma_start(k2_bits[:, :, :], k2.rearrange("(c p) f -> p c f", p=P)).then_inc(k2_loaded, 16)
            load_keep(0)
            load_x(1)
            load_keep(1)
            load_x(2)
            load_x_t(2)
            sp.wait_ge(x1_done, NT)
            move_x1(0)
            store_coords(1)
            load_coords(1)
            def body(n, norm, ahead):
                if ahead:
                    load_x(n + 3)
                if norm:
                    spread_norm(n + 2)
                    load_keep(n + 2)
                if ahead:
                    load_x_t(n + 3)
                store_y(n, 0)
                if norm:
                    store_coords(n + 2)
                    load_coords(n + 2)
                store_y(n, 1)

            def move_on(n):
                sp.wait_ge(y_stored, n * 32)
                sp.wait_ge(x1_done, n * NT + NT)
                move_x1(n)

            body(0, True, True)
            with sp.Fori(1, BATCHES - 3) as n:
                move_on(n)
                body(n, True, True)
            for n in range(BATCHES - 3, BATCHES - 1):
                move_on(n)
                body(n, n == BATCHES - 3, False)
            n = BATCHES - 1
            move_on(n)
            store_y(n, 0)
            for t in range(NT - 2, NT):
                sp.wait_ge(bank_free, n * USES + 2 * NF + t + FBANKS)
                sp.dma_start(tokens(out, n)[:, t:t + 1, :], y[:, t:t + 1, :]).then_inc(y_stored, 16)
            sp.wait_ge(y_stored, BATCHES * 32 + 16)

        @block.gpsimd
        def _(pool):
            def rstd1_of(i):
                pool.wait_ge(ve1_done, i * 1 + 1)
                nc.gpsimd.tensor_tensor(norm1[:, :, 1], ve1[:, :], neg_half[:, :], ALU.pow).then_inc(rstd1_done, 1)

            def rstd2_of(i):
                pool.wait_ge(ve2_done, i * 1 + 1)
                nc.gpsimd.tensor_tensor(rstd2[:, :], ve2[:, :], neg_half[:, :], ALU.pow).then_inc(rstd2_done, 1)

            def mask(i):
                for kt in KEY_ORDER:
                    pool.wait_ge(exp_done, i * 2 + (2 if kt == 0 else 1))
                    diagonal = probs[:, ROW[kt]:ROW[kt] + P]
                    nc.gpsimd.tensor_tensor(diagonal, diagonal, causal[:, :], ALU.mult).then_inc(masked, 1)

            def bias_x(i):
                pool.wait_ge(keep_loaded, i * 16 + 16)
                if not (isinstance(i, int) and i == 0):
                    pool.wait_ge(x1_done, i * NT)
                for t in range(NT):
                    nc.gpsimd.tensor_tensor(x_biased[:, t, :], x_keep[:, t, :], v_bias[:, :], ALU.add)\
                        .then_inc(biased, 1)

            def center(i):
                pool.wait_ge(norm_loaded, i * 16 - 16)
                pool.wait_ge(xt_loaded, i * 16 - 16)
                for c in range(ND):
                    nc.gpsimd.tensor_tensor(x_t[:, c, :], x_t[:, c, :], norm_wide[:, :, 0], ALU.subtract)\
                        .then_inc(centered, 1)

            def w0_tile(c):
                for half, to in enumerate((w0, w0_minus)):
                    nc.gpsimd.tensor_scalar(to[:, c, :], k0_bits[:, half * ND + c, :], w_factors[:, 0:1], 0.0,
                                            ALU.mult, ALU.add).then_inc(w0_scaled, 1)
                pool.wait_ge(w0_scaled, 2 * c + 2)
                nc.gpsimd.tensor_tensor(w0[:, c, :], w0[:, c, :], w0_minus[:, c, :], ALU.subtract)\
                    .then_inc(w0_made, 1)

            nc.gpsimd.memset(ident[:, :], 0.0).then_inc(filled, 1)
            nc.gpsimd.memset(neg_half[:, :], -0.5).then_inc(filled, 1)
            nc.gpsimd.memset(causal[:, :], 1.0).then_inc(filled, 1)
            nc.gpsimd.memset(pick[:, :, :], 0.0).then_inc(filled, 1)
            pool.wait_ge(filled, 1)
            nc.gpsimd.affine_select(out=ident[:, :], in_=ident[:, :], compare_op=ALU.not_equal, fill=1.0, base=0,
                                    pattern=[[-1, P]], channel_multiplier=1).then_inc(ident_made, 1)
            pool.wait_ge(ident_made, 1)
            nc.gpsimd.tensor_copy(identb[:, :], ident[:, :]).then_inc(ident_made, 1)
            rstd1_of(0)
            pool.wait_ge(filled, 4)
            nc.gpsimd.affine_select(out=causal[:, :], in_=causal[:, :], compare_op=ALU.is_ge, fill=0.0, base=0,
                                    pattern=[[1, P]], channel_multiplier=-1).then_inc(consts_made, 1)
            for part in range(PARTS):
                pool.wait_ge(consts_made, 1 + part)
                nc.gpsimd.affine_select(out=pick[:, :, :], in_=pick[:, :, :], compare_op=ALU.not_equal, fill=1.0,
                                        base=-COORDS * part, pattern=[[-1, COORDS], [0, P]],
                                        channel_multiplier=1).then_inc(consts_made, 1)
            pool.wait_ge(k1_loaded, 16)
            pool.wait_ge(factors_made, 3)
            for c in range(W1_ON_POOL):
                nc.gpsimd.tensor_scalar(w1[:, c, :], k1_bits[:, c, :], w_factors[:, 1:2], w_factors[:, 2:3],
                                        ALU.mult, ALU.add).then_inc(w1_made, 1)
            pool.wait_ge(k0_loaded, 16)
            w0_tile(0)
            pool.wait_ge(k2_loaded, 16)
            for c in range(0, NF, NF // 2):
                nc.gpsimd.tensor_scalar(w2[:, c:c + NF // 2, :], k2_bits[:, c:c + NF // 2, :], 2.0, -1.0,
                                        ALU.mult, ALU.add).then_inc(w2_made, 1)
            rstd1_of(1)
            mask(0)
            pool.wait_ge(v_bias_made, 1)
            bias_x(0)
            w0_tile(1)
            rstd2_of(0)

            def body(n, ahead):
                if ahead:
                    rstd1_of(n + 2)
                mask(n + 1)
                bias_x(n + 1)
                if ahead:
                    center(n + 2)
                rstd2_of(n + 1)

            with pool.Fori(0, BATCHES - 2) as n:
                body(n, True)
            body(BATCHES - 2, False)

        @block.scalar
        def _(act):
            def xn1_hi(i, banks=mbank):
                for c in range(ND):
                    if isinstance(i, int):
                        act.wait_ge(xn1_turned, i * ND + c + 1)
                    else:
                        act.wait_ge(xn_t_done, (i - 2) * ND + c + 1)
                    if c == 0 and not (isinstance(i, int) and i == 0):
                        act.wait_ge(v_summed, i * NT)
                    source = banks[c][:, :] if isinstance(i, int) else xn_t[:, c, :]
                    nc.scalar.activation(xn1_t[:, 0, c, :], source, ACT.Copy).then_inc(xn1_t_hi_done, 1)

            def v_hi(i, t, banks=2 * mbank):
                act.wait_ge(v_summed, i * NT + t + 1)
                if t == 0 and not (isinstance(i, int) and i == 0):
                    act.wait_ge(attn_summed, i * NT)
                nc.scalar.activation(v[:, 0, t, 0:D], banks[t][:, 0:D], ACT.Copy,
                                     scale=V_SCALE / (XN_SCALE * W_SCALE)).then_inc(v_hi_done, 1)

            def pos_t_out():
                act.wait_ge(pos_turned, 1)
                pt = mbank[0][0:PARTS * COORDS, 0:SEQ // 2].bitcast(BF16)
                nc.scalar.activation(pos_t[:, :], pt, ACT.Copy).then_inc(pos_t_done, 1)

            def squares(i, kt, coords=range(COORDS)):
                spread_on_pe = isinstance(i, int) and i == 0
                if kt == NT - 1 and 0 in coords:
                    act.wait_ge(pos_neg_done, i * 1 + 1)
                    if spread_on_pe:
                        act.wait_ge(coords_spread, 1)
                    else:
                        act.wait_ge(coords_loaded, i * 16)
                        act.wait_ge(sum_xyz_done, i * 2)
                n = SEQ - kt * P
                for c in coords:
                    wide = coord_bank[c] if spread_on_pe else coords_wide[:, :, c]
                    nc.scalar.activation(square[:, c, ROW[kt]:ROW[kt] + n], wide[:, kt * P:SEQ],
                                         ACT.Square, bias=pos_neg[:, kt, c:c + 1]).then_inc(squares_done, 1)

            def distance(i, h):
                act.wait_ge(sum_xyz_done, i * 2 + h + 1)
                a, b = CHUNKS[h]
                nc.scalar.activation(dist[:, a:b], sum_xyz[:, a:b], ACT.Sqrt).then_inc(dist_done, 1)

            def exponent(i, h):
                act.wait_ge(dist_done, i * 2 + h + 1)
                if h == 0 and not (isinstance(i, int) and i == 0):
                    act.wait_ge(probs_done, i * NT)
                a, b = CHUNKS[h]
                nc.scalar.activation(probs[:, a:b], dist[:, a:b], ACT.Exp, scale=-SCORE_SCALE).then_inc(exp_done, 1)

            def probs_high(i):
                for j, kt in enumerate(KEY_ORDER):
                    act.wait_ge(masked, i * NT + j + 1)
                    if j == 0 and not (isinstance(i, int) and i == 0):
                        act.wait_ge(attn_summed, i * NT)
                    row = slice(ROW[kt], ROW[kt] + SEQ - kt * P)
                    nc.scalar.activation(probs_hi[:, row], probs[:, row], ACT.Copy, scale=E_SCALE)\
                        .then_inc(probs_hi_done, 1)

            def h_hi(i):
                for c in range(ND):
                    act.wait_ge(xn2_turned, i * ND + c + 1)
                    nc.scalar.activation(h_t[:, 0, c, :], mbank[c][:, :], ACT.Copy).then_inc(h_hi_done, 1)

            def relu_hi(n, use):
                act.wait_ge(bank_summed, n * USES + use + 1)
                r = r0 if use < NF else r1
                nc.scalar.activation(r[:, 0, use % NF, :], fbank[use % FBANKS][:, :], ACT.Relu)\
                    .then_inc(relu_hi_done, 1)

            act.dma_start(small_rows[0:COORDS * ND, :], w3d.rearrange("c (a p) -> (c a) p", p=P))\
                .then_inc(small_loaded, 16)
            act.dma_start(small_rows[COORDS * ND:, :], bv.rearrange("(a p) -> a p", p=P)).then_inc(small_loaded, 16)
            act.dma_start(b3d_wide[:, :], spread(b3d)).then_inc(rows_loaded, 16)

            act.wait_ge(ones_made, 1)
            nc.scalar.activation(first_sqrt[:, :], ones_row[:, 0:1], ACT.Sqrt)
            for c in range(ND):
                act.wait_ge(wo_turned, c + 1)
                nc.scalar.activation(wo_t[:, c, :], mbank[c][:, 0:D], ACT.Copy).then_inc(wo_t_made, 1)
            xn1_hi(0)
            pos_t_out()
            squares(0, EARLY[0], range(COORDS - 1))
            for c in range(ND):
                act.wait_ge(powers_known, 2)
                nc.scalar.activation(wvo[:, 0, c, 0:D], fbank[1 + c][:, 0:D], ACT.Copy, scale=factors[:, 0, 0:1])\
                    .then_inc(weights_hi_made, 1)
            squares(0, EARLY[1], range(COORDS - 1))
            squares(0, 1, range(COORDS - 1))
            act.wait_ge(early_diff_done, len(EARLY))
            squares(0, 1, range(COORDS - 1, COORDS))
            squares(0, 0)
            v_hi(0, 0)
            v_hi(0, 1)
            distance(0, 0)
            distance(0, 1)
            exponent(0, 0)
            v_hi(0, 2)
            exponent(0, 1)
            v_hi(0, 3)
            probs_high(0)
            xn1_hi(1, early_turn_banks)
            act.wait_ge(k1_loaded, 16)
            act.wait_ge(factors_made, 3)
            for c in range(W1_ON_POOL, NF):
                nc.scalar.activation(w1[:, c, :], k1_bits[:, c, :], ACT.Identity, bias=w_factors[:, 2:3],
                                     scale=w_factors[:, 1:2]).then_inc(w1_made, 1)
            for t in range(2):
                v_hi(1, t, early_v_banks)
            h_hi(0)
            for t in range(2, NT):
                v_hi(1, t, early_v_banks)

            def body(n, attention, ahead):
                for m in range(NF):
                    relu_hi(n, m)
                if attention:
                    squares(n + 1, 3)
                    squares(n + 1, 2)
                relu_hi(n, NF)
                if attention:
                    squares(n + 1, 1)
                    squares(n + 1, 0)
                relu_hi(n, NF + 1)
                if attention:
                    distance(n + 1, 0)
                    distance(n + 1, 1)
                    exponent(n + 1, 0)
                    exponent(n + 1, 1)
                relu_hi(n, NF + 2)
                if attention:
                    probs_high(n + 1)
                for m in range(3, 7):
                    relu_hi(n, NF + m)
                if ahead:
                    xn1_hi(n + 2)
                relu_hi(n, NF + 7)
                if attention:
                    h_hi(n + 1)
                if ahead:
                    for t in range(NT):
                        v_hi(n + 2, t)

            with act.Fori(0, BATCHES - 2) as n:
                body(n, True, True)
            body(BATCHES - 2, True, False)
            body(BATCHES - 1, False, False)

        @block.vector
        def _(dve):
            def moments(i, stats, stats_done, mean, ve, part, part_done, scale, ve_done):
                dve.wait_ge(stats_done, i * NT + NT)
                nc.vector.tensor_tensor(part[:, 0, :], stats[:, :, 1], stats[:, :, 4], ALU.add).then_inc(part_done, 1)
                nc.vector.tensor_tensor(part[:, 1, :], stats[:, :, 1], stats[:, :, 4], ALU.subtract)\
                    .then_inc(part_done, 1)
                nc.vector.scalar_tensor_tensor(out=part[:, 2, :], in0=stats[:, :, 2], scalar=D * EPS,
                                               in1=stats[:, :, 5], op0=ALU.add, op1=ALU.add).then_inc(part_done, 1)
                dve.wait_ge(part_done, i * 5 + 2)
                nc.vector.scalar_tensor_tensor(out=part[:, 3, :], in0=part[:, 1, :], scalar=0.25 * scale,
                                               in1=part[:, 1, :], op0=ALU.mult, op1=ALU.mult).then_inc(part_done, 1)
                nc.vector.tensor_scalar(mean, part[:, 0, :], 0.5, None, ALU.mult).then_inc(part_done, 1)
                dve.wait_ge(part_done, i * 5 + 4)
                nc.vector.scalar_tensor_tensor(out=ve[:, :], in0=part[:, 2, :], scalar=scale / D,
                                               in1=part[:, 3, :], op0=ALU.mult, op1=ALU.add).then_inc(ve_done, 1)

            def ln1_stats(i, tiles=range(NT)):
                dve.wait_ge(x_loaded, i * 16 + 16)
                for t in tiles:
                    nc.vector.bn_stats(stats1[:, t, :], x_in[:, t, :]).then_inc(stats1_done, 1)

            def ln1_var(i):
                moments(i, stats1, stats1_done, norm1[:, :, 0], ve1, part1, part1_done, XN_SCALE ** -2, ve1_done)

            def normalize1(i):
                dve.wait_ge(rstd1_done, i * 1 + 1)
                dve.wait_ge(part1_done, i * 5 + 5)
                if not (isinstance(i, int) and i == 0):
                    dve.wait_ge(xn1_turned, i * ND)
                for t in range(NT):
                    nc.vector.tensor_scalar(xn1[:, t, :], x_in[:, t, :], norm1[:, t, 0:1], norm1[:, t, 1:2],
                                            ALU.subtract, ALU.mult).then_inc(xn1_done, 1)

            def normalize1_t(i):
                for c in range(ND):
                    dve.wait_ge(centered, (i - 2) * ND + c + 1)
                    nc.vector.tensor_tensor(xn_t[:, c, :], x_t[:, c, :], norm_wide[:, :, 1], ALU.mult)\
                        .then_inc(xn_t_done, 1)

            def xn1_lo(i, banks=mbank, tiles=range(ND)):
                for c in tiles:
                    dve.wait_ge(xn1_t_hi_done, i * ND + c + 1)
                    source = banks[c][:, :] if isinstance(i, int) else xn_t[:, c, :]
                    nc.vector.tensor_tensor(xn1_t[:, 1, c, :], source, xn1_t[:, 0, c, :], ALU.subtract)\
                        .then_inc(xn1_t_done, 1)

            def v_lo(i, t, banks=2 * mbank):
                dve.wait_ge(v_hi_done, i * NT + t + 1)
                nc.vector.scalar_tensor_tensor(out=v[:, 1, t, 0:D], in0=banks[t][:, 0:D],
                                               scalar=V_SCALE / (XN_SCALE * W_SCALE), in1=v[:, 0, t, 0:D],
                                               op0=ALU.mult, op1=ALU.subtract).then_inc(v_done, 1)

            def positions(i, t, sums, spread_bias, tiles):
                if t == 0 and not (isinstance(i, int) and i == 0):
                    dve.wait_ge(squares_done, squares_before(i))
                    if not (isinstance(i, int) and i == 1):
                        dve.wait_ge(coords_stored, i * 16 - 16)
                nc.vector.scalar_tensor_tensor(out=pos[:, t:t + tiles, :], in0=sums, scalar=factors[:, 1, 1:2],
                                               in1=spread_bias, op0=ALU.mult, op1=ALU.add).then_inc(pos_done, tiles)

            def positions_of(i, t, banks=2 * mbank):
                dve.wait_ge(v_summed, i * NT + t + 1)
                positions(i, t, banks[t][:, D:VC], b3d_wide[:, :], 1)

            def negate_pos(i):
                dve.wait_ge(pos_done, i * NT + NT)
                nc.vector.tensor_scalar(pos_neg[:, :, :], pos[:, :, :], -1.0, None, ALU.mult).then_inc(pos_neg_done, 1)

            def split_pos():
                nc.vector.tensor_copy(pos_parts[:, :, 0, :], pos[:, :, :]).then_inc(split_done, 1)
                for part in range(1, PARTS):
                    rest = pos if part == 1 else pos_rest[:, 0]
                    dve.wait_ge(split_done, 2 * part - 1)
                    nc.vector.tensor_tensor(pos_rest[:, part - 1], rest[:, :, :], pos_parts[:, :, part - 1, :],
                                            ALU.subtract).then_inc(split_done, 1)
                    dve.wait_ge(split_done, 2 * part)
                    nc.vector.tensor_copy(pos_parts[:, :, part, :], pos_rest[:, part - 1]).then_inc(split_done, 1)

            def early_squares(kt):
                if kt == EARLY[0]:
                    dve.wait_ge(coords_spread, 1)
                row = slice(ROW[kt], ROW[kt] + SEQ - kt * P)
                c = COORDS - 1
                diff = early_diff[:, ROW[kt] - ROW[EARLY[1]]:ROW[kt] - ROW[EARLY[1]] + SEQ - kt * P]
                nc.vector.tensor_scalar(diff, coord_bank[c][:, kt * P:SEQ], pos_neg[:, kt, c:c + 1],
                                        None, ALU.add).then_inc(early_diff_done, 1)
                dve.wait_ge(early_diff_done, EARLY.index(kt) + 1)
                nc.vector.tensor_tensor(square[:, c, row], diff, diff, ALU.mult)\
                    .then_inc(early_squares_done, 1)

            def sums(i, h):
                a, b = CHUNKS[h]
                if isinstance(i, int) and i == 0:
                    dve.wait_ge(early_squares_done, len(EARLY))
                dve.wait_ge(squares_done, squares_before(i + 1) - (COORDS if h == 0 else 0))
                nc.vector.scalar_tensor_tensor(out=sum_xy[:, a:b], in0=square[:, 0, a:b], scalar=TINY,
                                               in1=square[:, 1, a:b], op0=ALU.max, op1=ALU.add)\
                    .then_inc(sum_xy_done, 1)
                dve.wait_ge(sum_xy_done, i * 2 + h + 1)
                nc.vector.tensor_tensor(sum_xyz[:, a:b], sum_xy[:, a:b], square[:, 2, a:b], ALU.add)\
                    .then_inc(sum_xyz_done, 1)

            def probs_low(i):
                for j, kt in enumerate(KEY_ORDER):
                    dve.wait_ge(probs_hi_done, i * NT + j + 1)
                    row = slice(ROW[kt], ROW[kt] + SEQ - kt * P)
                    nc.vector.scalar_tensor_tensor(out=probs_lo[:, row], in0=probs[:, row], scalar=E_SCALE,
                                                   in1=probs_hi[:, row], op0=ALU.mult, op1=ALU.subtract)\
                        .then_inc(probs_done, 1)

            def softmax_factor(i, t):
                dve.wait_ge(attn_summed, i * NT + t + 1)
                nc.vector.reciprocal(rsum[:, 0, t:t + 1], mbank[t % 2][:, D:D + 1]).then_inc(rsum_done, 1)
                dve.wait_ge(rsum_done, i * 2 * NT + 2 * t + 1)
                nc.vector.tensor_scalar(rsum[:, 1, t:t + 1], rsum[:, 0, t:t + 1], factors[:, 0, 1:2], None, ALU.mult)\
                    .then_inc(rsum_done, 1)

            def residual(i, t):
                dve.wait_ge(biased, i * NT + t + 1)
                if t == 0 and not (isinstance(i, int) and i == 0):
                    dve.wait_ge(x1_moved, i * 16)
                dve.wait_ge(rsum_done, i * 2 * NT + 2 * t + 2)
                nc.vector.scalar_tensor_tensor(out=x1_new[:, t, :], in0=mbank[t % 2][:, 0:D],
                                               scalar=rsum[:, 1, t:t + 1], in1=x_biased[:, t, :],
                                               op0=ALU.mult, op1=ALU.add).then_inc(x1_done, 1)

            def ln2_stats(i, t):
                dve.wait_ge(x1_done, i * NT + t + 1)
                nc.vector.bn_stats(stats2[:, t, :], x1_new[:, t, :]).then_inc(stats2_done, 1)

            def ln2_var(i):
                moments(i, stats2, stats2_done, mean2[:, :], ve2, part2, part2_done, XN_SCALE ** -2, ve2_done)

            def normalize2(i):
                dve.wait_ge(rstd2_done, i * 1 + 1)
                dve.wait_ge(part2_done, i * 5 + 5)
                if not (isinstance(i, int) and i == 0):
                    dve.wait_ge(xn2_turned, i * ND)
                for t in range(NT):
                    nc.vector.tensor_scalar(xn2[:, t, :], x1_new[:, t, :], mean2[:, t:t + 1], rstd2[:, t:t + 1],
                                            ALU.subtract, ALU.mult).then_inc(xn2_done, 1)

            def h_lo(i):
                for c in range(ND):
                    dve.wait_ge(h_hi_done, i * ND + c + 1)
                    nc.vector.tensor_tensor(h_t[:, 1, c, :], mbank[c][:, :], h_t[:, 0, c, :], ALU.subtract)\
                        .then_inc(h_done, 1)

            def relu_lo(n, use):
                r = r0 if use < NF else r1
                dve.wait_ge(relu_hi_done, n * 2 * NF + use + 1)
                nc.vector.scalar_tensor_tensor(out=r[:, 1, use % NF, :], in0=fbank[use % FBANKS][:, :], scalar=0.0,
                                               in1=r[:, 0, use % NF, :], op0=ALU.max, op1=ALU.subtract)\
                    .then_inc(bank_free, 1)

            def finish(n, half):
                use = 2 * NF + half
                dve.wait_ge(bank_summed, n * USES + use + 1)
                if half == 0:
                    dve.wait_ge(x1_moved, n * 16 + 16)
                t = 2 * half
                z = fbank[use % FBANKS][:, :].rearrange("p (t d) -> p t d", d=D)
                nc.vector.scalar_tensor_tensor(out=y[:, t:t + 2, :], in0=z, scalar=out_factor[:, 1:2],
                                               in1=x1_cur[:, t:t + 2, :], op0=ALU.mult, op1=ALU.add)\
                    .then_inc(bank_free, 1)

            def finish_last(t):
                dve.wait_ge(bank_summed, (BATCHES - 1) * USES + 2 * NF + t)
                bank = fbank[(USES - 1) % FBANKS] if t == NT - 2 else coord_bank[0]
                nc.vector.scalar_tensor_tensor(out=y[:, t, :], in0=bank[:, (t % 2) * D:(t % 2 + 1) * D],
                                               scalar=out_factor[:, 1:2], in1=x1_cur[:, t, :],
                                               op0=ALU.mult, op1=ALU.add)\
                    .then_inc(bank_free, 1)

            def powers_of(j):
                dve.wait_ge(largest_turned, 2 - j)
                row = largest_row[:, j:j + 1]
                up, down = powers[:, j, 0:1], powers[:, j, 1:2]
                at = (1 - j) * 5
                nc.vector.reduce_max(row, fbank[0][0:1, 0:P], AX_X).then_inc(power_steps, 1)
                dve.wait_ge(power_steps, at + 1)
                nc.vector.tensor_scalar(row, row, TINY, None, ALU.max).then_inc(power_steps, 1)
                dve.wait_ge(power_steps, at + 2)
                nc.vector.tensor_scalar(down.bitcast(I32), row.bitcast(I32), 0xFF << 23, None, ALU.bitwise_and)\
                    .then_inc(power_steps, 1)
                dve.wait_ge(power_steps, at + 3)
                nc.vector.tensor_scalar(up.bitcast(I32), down.bitcast(I32), -1.0, float(254 << 23),
                                        ALU.mult, ALU.add).then_inc(power_steps, 1)
                dve.wait_ge(power_steps, at + 4)
                nc.vector.tensor_scalar(up, up, W_SCALE, None, ALU.mult)
                nc.vector.tensor_scalar(down, down, 1.0 / V_SCALE if j == 0 else 1.0 / (XN_SCALE * W_SCALE), None,
                                        ALU.mult).then_inc(power_steps, 1)

            def take_factors(j):
                dve.wait_ge(powers_spread, 2 - j)
                nc.vector.tensor_copy(factors[:, j, :], fbank[0][:, P:P + 2]).then_inc(powers_known, 1)

            nc.vector.memset(ones_row[:, :], 1.0).then_inc(ones_made, 1)
            nc.vector.memset(v[:, 1, :, D:D + 1], 0.0).then_inc(ones_made, 1)
            nc.vector.memset(v[:, 0, :, D:D + 1], 1.0).then_inc(bank_free, FBANKS)
            dve.wait_ge(half_loaded, 16)
            for t in range(NT // 2):
                nc.vector.bn_stats(stats1[:, t, :], x_in[:, t, :]).then_inc(stats1_done, 1)
            ln1_stats(0, range(NT // 2, NT))
            ln1_var(0)
            dve.wait_ge(small_turned, 1)
            nc.vector.tensor_copy(small_cols[:, :], fbank[0][:, 0:ND * (COORDS + 1)]).then_inc(small_made, 1)
            dve.wait_ge(small_made, 1)
            nc.vector.tensor_reduce(largest[:, 1:2], small_cols[:, 0:ND * COORDS], AX_X, ALU.max,
                                    apply_absolute_value=True).then_inc(largest_found, 1)
            for c in range(ND):
                j = ND * COORDS + c
                nc.vector.tensor_copy(bv_wide[:, c, :], small_cols[:, j:j + 1].to_broadcast([P, P]))\
                    .then_inc(bv_spread, 1)
            normalize1(0)
            powers_of(1)
            dve.wait_ge(scales_loaded, 48)
            nc.vector.tensor_scalar(signs[:, :], scales[:, 0:2], 0.0, 2.0, ALU.is_ge, ALU.mult).then_inc(signs_made, 1)
            dve.wait_ge(signs_made, 1)
            nc.vector.tensor_scalar(signs[:, :], signs[:, :], -1.0, None, ALU.add).then_inc(signs_made, 1)
            dve.wait_ge(signs_made, 2)
            nc.vector.tensor_tensor(magnitudes[:, :], scales[:, 0:2], signs[:, :], ALU.mult).then_inc(signs_made, 1)
            nc.vector.tensor_scalar(w_factors[:, 0:1], signs[:, 0:1], 2.0 * W0_SCALE, None, ALU.mult)\
                .then_inc(factors_made, 1)
            nc.vector.tensor_scalar(w_factors[:, 1:2], signs[:, 1:2], 2.0 * W1_SCALE, None, ALU.mult)\
                .then_inc(factors_made, 1)
            nc.vector.tensor_scalar(w_factors[:, 2:3], signs[:, 1:2], -W1_SCALE, None, ALU.mult)\
                .then_inc(factors_made, 1)
            take_factors(1)
            dve.wait_ge(powers_known, 1)
            w3d_in = small_cols[:, 0:ND * COORDS].rearrange("p (c a) -> p a c", a=ND)
            nc.vector.tensor_scalar(wvo[:, 0, :, D:VC], w3d_in, factors[:, 1, 0:1], None, ALU.mult)\
                .then_inc(w3d_made, 1)
            dve.wait_ge(w3d_made, 1)
            nc.vector.scalar_tensor_tensor(out=wvo[:, 1, :, D:VC], in0=w3d_in, scalar=factors[:, 1, 0:1],
                                           in1=wvo[:, 0, :, D:VC], op0=ALU.mult, op1=ALU.subtract)\
                .then_inc(w3d_made, 1)
            xn1_lo(0)
            for c in range(ND):
                dve.wait_ge(wvo_summed, c + 1)
                nc.vector.tensor_reduce(largest_of_tile[:, c:c + 1], fbank[1 + c][:, 0:D], AX_X, ALU.max,
                                        apply_absolute_value=True).then_inc(abs_done, 1)
            dve.wait_ge(abs_done, ND)
            nc.vector.reduce_max(largest[:, 0:1], largest_of_tile[:, :], AX_X).then_inc(largest_found, 1)
            dve.wait_ge(rows_loaded, 32)
            dve.wait_ge(pos_summed, 1)
            positions(0, 0, fbank[0][:, 2 * P:2 * P + NT * COORDS].rearrange("p (t c) -> p t c", c=COORDS),
                      b3d_wide[:, :].rearrange("p (a c) -> p a c", a=1).to_broadcast([P, NT, COORDS]), NT)
            negate_pos(0)
            split_pos()
            powers_of(0)
            take_factors(0)
            early_squares(EARLY[0])
            for c in range(ND):
                dve.wait_ge(weights_hi_made, c + 1)
                nc.vector.scalar_tensor_tensor(out=wvo[:, 1, c, 0:D], in0=fbank[1 + c][:, 0:D],
                                               scalar=factors[:, 0, 0:1], in1=wvo[:, 0, c, 0:D],
                                               op0=ALU.mult, op1=ALU.subtract).then_inc(wvo_made, 1)
            early_squares(EARLY[1])
            ln1_stats(1, range(NT // 2))
            sums(0, 0)
            sums(0, 1)
            ln1_stats(1, range(NT // 2, NT))
            ln1_var(1)
            v_lo(0, 0)
            v_lo(0, 1)
            dve.wait_ge(signs_made, 3)
            nc.vector.scalar_tensor_tensor(out=out_factor[:, 0:1], in0=magnitudes[:, 0:1], scalar=OUT_SCALE,
                                           in1=magnitudes[:, 1:2], op0=ALU.mult, op1=ALU.mult)\
                .then_inc(out_factor_made, 1)
            dve.wait_ge(out_factor_made, 1)
            nc.vector.tensor_tensor(out_factor[:, 1:2], out_factor[:, 0:1], scales[:, 2:3], ALU.mult)\
                .then_inc(out_factor_made, 1)
            dve.wait_ge(out_factor_made, 2)
            normalize1(1)
            v_lo(0, 2)
            dve.wait_ge(wvo_summed, ND + 1)
            nc.vector.tensor_tensor(v_bias[:, :], fbank[0][:, D:2 * D], bo_wide[:, :], ALU.add)\
                .then_inc(v_bias_made, 1)
            v_lo(0, 3)
            probs_low(0)
            xn1_lo(1, early_turn_banks, [0])
            softmax_factor(0, 0)
            for t in range(NT):
                residual(0, t)
                if t < NT - 1:
                    softmax_factor(0, t + 1)
                ln2_stats(0, t)
            ln2_var(0)
            xn1_lo(1, early_turn_banks, [1])
            normalize2(0)
            for t in range(2):
                v_lo(1, t, early_v_banks)
                positions_of(1, t, early_v_banks)
            h_lo(0)
            for t in range(2, NT):
                v_lo(1, t, early_v_banks)
                positions_of(1, t, early_v_banks)
            negate_pos(1)

            def body(n, attention, ahead):
                for m in range(NF):
                    relu_lo(n, m)
                if ahead:
                    ln1_stats(n + 2)
                    ln1_var(n + 2)
                relu_lo(n, NF)
                if attention:
                    sums(n + 1, 0)
                    sums(n + 1, 1)
                relu_lo(n, NF + 1)
                relu_lo(n, NF + 2)
                if attention:
                    probs_low(n + 1)
                relu_lo(n, NF + 3)
                relu_lo(n, NF + 4)
                if attention:
                    for t in range(2):
                        softmax_factor(n + 1, t)
                        residual(n + 1, t)
                        ln2_stats(n + 1, t)
                relu_lo(n, NF + 5)
                if attention:
                    for t in range(2, NT):
                        softmax_factor(n + 1, t)
                        residual(n + 1, t)
                        ln2_stats(n + 1, t)
                    ln2_var(n + 1)
                if ahead:
                    normalize1_t(n + 2)
                relu_lo(n, NF + 6)
                if attention:
                    normalize2(n + 1)
                if ahead:
                    xn1_lo(n + 2)
                relu_lo(n, NF + 7)
                if attention:
                    h_lo(n + 1)
                finish(n, 0)
                if ahead:
                    for t in range(NT):
                        v_lo(n + 2, t)
                        positions_of(n + 2, t)
                    negate_pos(n + 2)
                if attention:
                    finish(n, 1)
                else:
                    finish_last(NT - 2)
                    finish_last(NT - 1)

            with dve.Fori(0, BATCHES - 2) as n:
                body(n, True, True)
            body(BATCHES - 2, True, False)
            body(BATCHES - 1, False, False)

        @block.tensor
        def _(pe):
            def turn_xn1(i, banks=mbank):
                pe.wait_ge(xn1_done, i * NT + NT)
                for c in range(ND):
                    for t in range(NT):
                        last = nc.tensor.transpose(banks[c][:, t * P:(t + 1) * P], xn1[:, t, c * P:(c + 1) * P],
                                                   ident[:, :])
                    last.then_inc(xn1_turned, 1)

            PASSES = ((0, 0), (0, 1), (1, 0))

            def values(i, t, columns=VC, banks=2 * mbank):
                if t == 0:
                    pe.wait_ge(xn1_t_done, i * ND + ND)
                if banks[t] in banks[:t]:
                    pe.wait_ge(v_done, i * NT + t - 1)
                    if columns > D:
                        pe.wait_ge(pos_done, i * NT + t - 1)
                for c in range(ND):
                    for a, b in PASSES:
                        last = nc.tensor.matmul(banks[t][:, 0:columns], xn1_t[:, a, c, t * P:(t + 1) * P],
                                                wvo[:, b, c, 0:columns], start=(c == 0 and (a, b) == (0, 0)),
                                                stop=(c == ND - 1 and (a, b) == PASSES[-1]))
                last.then_inc(v_summed, 1)

            def turn_pos():
                pe.wait_ge(split_done, 2 * PARTS - 1)
                pt = mbank[0][0:PARTS * COORDS, 0:SEQ // 2].bitcast(BF16)
                for t in range(NT):
                    last = nc.tensor.transpose(pt[:, t * P:(t + 1) * P],
                                               pos_parts[:, t].rearrange("p a c -> p (a c)"), identb[:, :])
                last.then_inc(pos_turned, 1)

            def spread_coords():
                pe.wait_ge(pos_t_done, 1)
                for c in range(COORDS):
                    last = nc.tensor.matmul(coord_bank[c][:, :], pick[:, c, :], pos_t[:, :], start=True, stop=True)
                last.then_inc(coords_spread, 1)

            def attend(i, qt):
                if qt == 0:
                    pe.wait_ge(probs_done, i * NT + NT)
                    pe.wait_ge(v_done, i * NT + NT)
                if qt >= 2:
                    pe.wait_ge(x1_done, i * NT + qt - 1)
                for kt in range(qt + 1):
                    col = ROW[kt] + (qt - kt) * P
                    for a, b in PASSES:
                        e = (probs_hi, probs_lo)[a]
                        last = nc.tensor.matmul(mbank[qt % 2][:, 0:D + 1], e[:, col:col + P], v[:, b, kt, :],
                                                start=(kt == 0 and (a, b) == (0, 0)),
                                                stop=(kt == qt and (a, b) == PASSES[-1]))
                last.then_inc(attn_summed, 1)

            def turn_xn2(i):
                for c in range(ND):
                    for t in range(NT):
                        if c == 0:
                            pe.wait_ge(xn2_done, i * NT + t + 1)
                        last = nc.tensor.transpose(mbank[c][:, t * P:(t + 1) * P], xn2[:, t, c * P:(c + 1) * P],
                                                   ident[:, :])
                    last.then_inc(xn2_turned, 1)

            def hidden(n, use, weights, source, k_tiles):
                m = use % NF
                if m or weights is w0:
                    pe.wait_ge(bank_free, n * USES + use + 1)
                for k in range(k_tiles):
                    if weights is w0 and m == 0:
                        pe.wait_ge(h_done, n * ND + k + 1)
                    if weights is w1 and m == 0:
                        pe.wait_ge(bank_free, n * USES + max(k, use - FBANKS) + 1 + FBANKS)
                    for part in range(2):
                        last = nc.tensor.matmul(fbank[use % FBANKS][:, :], weights[:, k, m * P:(m + 1) * P],
                                                source[:, part, k, :], start=(k == 0 and part == 0),
                                                stop=(k == k_tiles - 1 and part == 1))
                last.then_inc(bank_summed, 1)

            def layer0(n, m):
                hidden(n, m, w0, h_t, ND)

            def layer1(n, m):
                hidden(n, NF + m, w1, r0, NF)

            def layer2(n, half, tiles=(0, 1), bank=None):
                use = 2 * NF + half
                if half == 1 and 0 in tiles:
                    pe.wait_ge(bank_free, n * USES + use + 1)
                for s in tiles:
                    t = 2 * half + s
                    target = fbank[use % FBANKS] if bank is None else bank
                    for k in range(NF):
                        if half == 0 and s == 0:
                            pe.wait_ge(bank_free, n * USES + NF + max(k, NF - FBANKS) + 1 + FBANKS)
                        for part in range(2):
                            last = nc.tensor.matmul(target[:, s * D:(s + 1) * D],
                                                    r1[:, part, k, t * P:(t + 1) * P], w2[:, k, :],
                                                    start=(k == 0 and part == 0), stop=(k == NF - 1 and part == 1))
                if 1 in tiles or bank is not None:
                    last.then_inc(bank_summed, 1)

            def turn_largest(j):
                pe.wait_ge(largest_found, 2 - j)
                nc.tensor.transpose(fbank[0][0:1, 0:P], largest[:, j:j + 1], ident[:, :]).then_inc(largest_turned, 1)

            def spread_powers(j):
                pe.wait_ge(power_steps, (2 - j) * 5)
                nc.tensor.matmul(fbank[0][:, P:P + 2], ones_row[:, :], powers[:, j, :], start=True, stop=True)\
                    .then_inc(powers_spread, 1)

            def keep_warm(bank, times):
                wide = identb[:, :].rearrange("p (a n) -> p a n", a=1).to_broadcast([P, SEQ // P, P])
                for _ in range(times):
                    nc.tensor.matmul(bank[:, :].rearrange("p (a n) -> p a n", n=P), identb[:, :], wide,
                                     start=True, stop=True)

            def wvo_tile(c):
                for j in range(ND):
                    last = nc.tensor.matmul(fbank[1 + c][:, 0:D], wv_rows[:, j, c * P:(c + 1) * P], wo_t[:, j, :],
                                            start=(j == 0), stop=(j == ND - 1))
                last.then_inc(wvo_summed, 1)

            pe.wait_ge(ident_made, 2)
            keep_warm(coord_bank[2], 6)
            pe.wait_ge(small_loaded, 32)
            nc.tensor.transpose(fbank[0][:, 0:ND * (COORDS + 1)], small_rows[:, :],
                                ident[0:ND * (COORDS + 1), 0:ND * (COORDS + 1)]).then_inc(small_turned, 1)
            pe.wait_ge(wo_loaded, 16)
            for c in range(ND):
                for o in range(ND):
                    last = nc.tensor.transpose(mbank[c][:, o * P:(o + 1) * P], wo_rows[:, o, c * P:(c + 1) * P],
                                               ident[:, :])
                last.then_inc(wo_turned, 1)
            turn_largest(1)
            pe.wait_ge(wo_t_made, ND)
            pe.wait_ge(wv_loaded, 16)
            wvo_tile(0)
            turn_xn1(0)
            pe.wait_ge(ones_made, 2)
            spread_powers(1)
            wvo_tile(1)
            keep_warm(coord_bank[2], 4)
            pe.wait_ge(w3d_made, 2)
            pe.wait_ge(xn1_t_done, ND)
            for t in range(NT):
                at = 2 * P + t * COORDS
                for c in range(ND):
                    for a, b in PASSES:
                        last = nc.tensor.matmul(fbank[0][:, at:at + COORDS], xn1_t[:, a, c, t * P:(t + 1) * P],
                                                wvo[:, b, c, D:VC], start=(c == 0 and (a, b) == (0, 0)),
                                                stop=(c == ND - 1 and (a, b) == PASSES[-1]))
            last.then_inc(pos_summed, 1)
            pe.wait_ge(pos_done, NT)
            turn_largest(0)
            keep_warm(coord_bank[2], 4)
            turn_pos()
            pe.wait_ge(consts_made, 1 + PARTS)
            spread_coords()
            spread_powers(0)
            keep_warm(mbank[1], 6)
            pe.wait_ge(wvo_made, ND)
            pe.wait_ge(pos_t_done, 1)
            for t in range(2):
                values(0, t, D)
            pe.wait_ge(bv_spread, ND)
            for j in range(ND):
                last = nc.tensor.matmul(fbank[0][:, D:2 * D], bv_wide[:, j, :], wo_t[:, j, :],
                                        start=(j == 0), stop=(j == ND - 1))
            last.then_inc(wvo_summed, 1)
            keep_warm(fbank[1], 12)
            for t in range(2, NT):
                values(0, t, D)
            pe.wait_ge(squares_done, squares_before(1))
            pe.wait_ge(early_squares_done, len(EARLY))
            keep_warm(coord_bank[2], 4)
            turn_xn1(1, early_turn_banks)
            keep_warm(coord_bank[2], 2)
            for qt in range(NT):
                attend(0, qt)
            keep_warm(coord_bank[2], 12)
            for t in range(2):
                values(1, t, banks=early_v_banks)
            pe.wait_ge(x1_done, NT)
            turn_xn2(0)
            for t in range(2, NT):
                values(1, t, banks=early_v_banks)
            pe.wait_ge(v_bias_made, 1)
            pe.wait_ge(w0_made, ND)
            pe.wait_ge(w1_made, NF)
            pe.wait_ge(w2_made, 2)

            def body(n, attention, ahead):
                for m in range(NF):
                    layer0(n, m)
                for m in range(0, 5):
                    layer1(n, m)
                if attention:
                    attend(n + 1, 0)
                    attend(n + 1, 1)
                layer1(n, 5)
                if attention:
                    attend(n + 1, 2)
                    attend(n + 1, 3)
                layer1(n, 6)
                layer1(n, 7)
                if attention:
                    pe.wait_ge(x1_done, n * NT + 2 * NT)
                    turn_xn2(n + 1)
                layer2(n, 0)
                if ahead:
                    pe.wait_ge(h_done, n * ND + 2 * ND)
                    values(n + 2, 0)
                    values(n + 2, 1)
                layer2(n, 1, [0], None if attention else fbank[(USES - 1) % FBANKS])
                if ahead:
                    values(n + 2, 2)
                    values(n + 2, 3)
                layer2(n, 1, [1], None if attention else coord_bank[0])

            with pe.Fori(0, BATCHES - 2) as n:
                body(n, True, True)
            body(BATCHES - 2, True, False)
            body(BATCHES - 1, False, False)


INPUTS = ["L0_attn_x", "L0_attn_wv", "L0_attn_bv", "L0_attn_wo", "L0_attn_bo", "L0_attn_w3d", "L0_attn_b3d",
          "L0_ffn_k0", "L0_ffn_k1", "L0_ffn_k2", "L0_ffn_s0", "L0_ffn_s1", "L0_ffn_s2"]


def kernel(**inputs):
    import numpy as np
    import concourse.bacc as bacc
    from concourse.bass_utils import run_bass_kernel_spmd

    nc = bacc.Bacc("TRN2", target_bir_lowering=False, num_devices=1)
    arrays, args = {}, []
    for name in INPUTS:
        a = np.ascontiguousarray(inputs[name])
        if a.ndim == 0:
            a = a.reshape(1)
        layouts = {name: a, name + "_turned": np.ascontiguousarray(a.transpose(0, 2, 1))} if a.ndim == 3 else {name: a}
        for key, b in layouts.items():
            arrays[key + "_dram"] = b
            args.append(nc.dram_tensor(key + "_dram", b.shape, mybir.dt.from_np(b.dtype), kind="ExternalInput").ap())
    shape = inputs["L0_attn_x"].shape
    args.append(nc.dram_tensor("coords_dram", (*shape[:2], inputs["L0_attn_w3d"].shape[0]), F32).ap())
    args.append(nc.dram_tensor("norms_dram", (*shape[:2], 2), F32).ap())
    args.append(nc.dram_tensor("out_dram", shape, F32, kind="ExternalOutput").ap())
    block_kernel(nc, *args)
    result = run_bass_kernel_spmd(nc, [arrays], core_ids=[0])
    return result.results[0]["out_dram"]
```
